# Optimizing a Trainium2 kernel written in Bass

```python
import numpy as np
import jax
import jax.numpy as jnp

def _softmax(x, axis=-1):
    return jax.nn.softmax(x, axis=axis)

def _gelu(x):
    return jax.nn.gelu(x, approximate=True)

def _silu(x):
    return jax.nn.silu(x)

def _sigmoid(x):
    return jax.nn.sigmoid(x)

def _layernorm(x, axis=-1, eps=1e-05):
    m = jnp.mean(x, axis=axis, keepdims=True)
    v = jnp.var(x, axis=axis, keepdims=True)
    return (x - m) / jnp.sqrt(v + eps)

def _scatter_add(tgt, idx, src, axis=0):
    return tgt.at[idx].add(src)

def _segment_sum(src, seg, n):
    return jax.ops.segment_sum(src, seg, n)
kernel_name = 'mk_seq_postln_d1_jaxref_r8_94121f'

def setup_inputs(seed: int=0):
    np.random.seed(seed)
    _w = jnp.asarray

    def _L0_attn_setup():
        import jax, jax.numpy as jnp
        import numpy as np

        def _silu(x):
            return x * jax.nn.sigmoid(x)

        def _mamba_dir(h, W_in, conv_w, conv_b, Wx, Wdt, bdt, A_log, Dp, W_out):
            Bsz, L, Dm = h.shape
            Di = W_in.shape[0] // 2
            N = A_log.shape[1]
            K = conv_w.shape[1]
            dt_rank = Wdt.shape[1]
            xz = jnp.einsum('bld,ed->ble', h, W_in)
            x, z = (xz[..., :Di], xz[..., Di:])
            xc = jnp.transpose(x, (0, 2, 1))
            xc = jax.lax.conv_general_dilated(xc, conv_w[:, None, :], window_strides=(1,), padding=[(K - 1, 0)], dimension_numbers=('NCH', 'OIH', 'NCH'), feature_group_count=Di)
            x = _silu(jnp.transpose(xc, (0, 2, 1)) + conv_b[None, None, :])
            x_dbl = jnp.einsum('bld,ed->ble', x, Wx)
            dt = x_dbl[..., :dt_rank]
            Bm = x_dbl[..., dt_rank:dt_rank + N]
            Cm = x_dbl[..., dt_rank + N:]
            dt = jax.nn.softplus(jnp.einsum('blr,dr->bld', dt, Wdt) + bdt)
            A = -jnp.exp(A_log)
            dA = jnp.exp(dt[..., None] * A)
            dBx = (dt * x)[..., None] * Bm[:, :, None, :]

            def step(hc, inp):
                dA_t, dBx_t, C_t = inp
                hc = dA_t * hc + dBx_t
                return (hc, jnp.einsum('bdn,bn->bd', hc, C_t))
            h0 = jnp.zeros((Bsz, Di, N), dtype=x.dtype)
            _, ys = jax.lax.scan(step, h0, (jnp.moveaxis(dA, 1, 0), jnp.moveaxis(dBx, 1, 0), jnp.moveaxis(Cm, 1, 0)))
            y = jnp.moveaxis(ys, 0, 1) + x * Dp
            y = y * _silu(z)
            return jnp.einsum('bld,ed->ble', y, W_out)
        key = jax.random.key(seed)
        ks = jax.random.split(key, 16)
        B, L, Dm = (1, 256, 128)
        Di, N, Kc, R = (256, 16, 4, 64)
        s = 0.02
        inp = {'hidden_states': jax.random.normal(ks[0], (B, L, Dm), jnp.float32), 'W_in': jax.random.normal(ks[1], (2 * Di, Dm), jnp.float32) * s, 'W_out': jax.random.normal(ks[2], (Dm, Di), jnp.float32) * s}
        a_log = jnp.log(jnp.broadcast_to(jnp.arange(1, N + 1, dtype=jnp.float32), (Di, N)))
        for i, d in enumerate(['fwd', 'rev']):
            o = 3 + 6 * i
            inp[f'conv_w_{d}'] = jax.random.normal(ks[o + 0], (Di, Kc), jnp.float32) * 0.2
            inp[f'conv_b_{d}'] = jnp.zeros((Di,), jnp.float32)
            inp[f'Wx_{d}'] = jax.random.normal(ks[o + 1], (R + 2 * N, Di), jnp.float32) * s
            inp[f'Wdt_{d}'] = jax.random.normal(ks[o + 2], (Di, R), jnp.float32) * s
            inp[f'bdt_{d}'] = jnp.full((Di,), -4.6, jnp.float32)
            inp[f'A_log_{d}'] = a_log
            inp[f'D_{d}'] = jnp.ones((Di,), jnp.float32)
        return inp
    _L0_attn_in = _L0_attn_setup()

    def _L0_ffn_setup():
        import jax, jax.numpy as jnp
        import numpy as np
        LN_EPS = 0.001
        EPS = 1e-05
        QB = 128.0

        def ste_round(x):
            return x + jax.lax.stop_gradient(jnp.round(x) - x)
        key = jax.random.key(seed)
        k1, k2 = jax.random.split(key)
        x = jax.random.normal(k1, (4, 1024, 128), dtype=jnp.float32)
        weight = jax.random.normal(k2, (128, 128), dtype=jnp.float32) * 0.02
        ln_gamma = jnp.ones((128,), dtype=jnp.float32)
        ln_beta = jnp.zeros((128,), dtype=jnp.float32)
        return {'x': x, 'weight': weight, 'ln_gamma': ln_gamma, 'ln_beta': ln_beta}
    _L0_ffn_in = _L0_ffn_setup()
    _d = {'L0_attn_hidden_states': _L0_attn_in['hidden_states'], 'L0_attn_W_in': _L0_attn_in['W_in'], 'L0_attn_W_out': _L0_attn_in['W_out'], 'L0_attn_conv_w_fwd': _L0_attn_in['conv_w_fwd'], 'L0_attn_conv_b_fwd': _L0_attn_in['conv_b_fwd'], 'L0_attn_Wx_fwd': _L0_attn_in['Wx_fwd'], 'L0_attn_Wdt_fwd': _L0_attn_in['Wdt_fwd'], 'L0_attn_bdt_fwd': _L0_attn_in['bdt_fwd'], 'L0_attn_A_log_fwd': _L0_attn_in['A_log_fwd'], 'L0_attn_D_fwd': _L0_attn_in['D_fwd'], 'L0_attn_conv_w_rev': _L0_attn_in['conv_w_rev'], 'L0_attn_conv_b_rev': _L0_attn_in['conv_b_rev'], 'L0_attn_Wx_rev': _L0_attn_in['Wx_rev'], 'L0_attn_Wdt_rev': _L0_attn_in['Wdt_rev'], 'L0_attn_bdt_rev': _L0_attn_in['bdt_rev'], 'L0_attn_A_log_rev': _L0_attn_in['A_log_rev'], 'L0_attn_D_rev': _L0_attn_in['D_rev'], 'L0_ffn_weight': _L0_ffn_in['weight'], 'L0_ffn_ln_gamma': _L0_ffn_in['ln_gamma'], 'L0_ffn_ln_beta': _L0_ffn_in['ln_beta']}
    _x0 = _d['L0_attn_hidden_states']
    _d['L0_attn_hidden_states'] = jax.random.normal(jax.random.fold_in(jax.random.key(seed), 1), (4, 1024, 128), dtype=_x0.dtype)
    del _x0
    return _d

def reference(L0_attn_hidden_states, L0_attn_W_in, L0_attn_W_out, L0_attn_conv_w_fwd, L0_attn_conv_b_fwd, L0_attn_Wx_fwd, L0_attn_Wdt_fwd, L0_attn_bdt_fwd, L0_attn_A_log_fwd, L0_attn_D_fwd, L0_attn_conv_w_rev, L0_attn_conv_b_rev, L0_attn_Wx_rev, L0_attn_Wdt_rev, L0_attn_bdt_rev, L0_attn_A_log_rev, L0_attn_D_rev, L0_ffn_weight, L0_ffn_ln_gamma, L0_ffn_ln_beta):

    def _L0_attn_ref(hidden_states, W_in, W_out, conv_w_fwd, conv_b_fwd, Wx_fwd, Wdt_fwd, bdt_fwd, A_log_fwd, D_fwd, conv_w_rev, conv_b_rev, Wx_rev, Wdt_rev, bdt_rev, A_log_rev, D_rev):
        import jax, jax.numpy as jnp
        import numpy as np

        def _silu(x):
            return x * jax.nn.sigmoid(x)

        def _mamba_dir(h, W_in, conv_w, conv_b, Wx, Wdt, bdt, A_log, Dp, W_out):
            Bsz, L, Dm = h.shape
            Di = W_in.shape[0] // 2
            N = A_log.shape[1]
            K = conv_w.shape[1]
            dt_rank = Wdt.shape[1]
            xz = jnp.einsum('bld,ed->ble', h, W_in)
            x, z = (xz[..., :Di], xz[..., Di:])
            xc = jnp.transpose(x, (0, 2, 1))
            xc = jax.lax.conv_general_dilated(xc, conv_w[:, None, :], window_strides=(1,), padding=[(K - 1, 0)], dimension_numbers=('NCH', 'OIH', 'NCH'), feature_group_count=Di)
            x = _silu(jnp.transpose(xc, (0, 2, 1)) + conv_b[None, None, :])
            x_dbl = jnp.einsum('bld,ed->ble', x, Wx)
            dt = x_dbl[..., :dt_rank]
            Bm = x_dbl[..., dt_rank:dt_rank + N]
            Cm = x_dbl[..., dt_rank + N:]
            dt = jax.nn.softplus(jnp.einsum('blr,dr->bld', dt, Wdt) + bdt)
            A = -jnp.exp(A_log)
            dA = jnp.exp(dt[..., None] * A)
            dBx = (dt * x)[..., None] * Bm[:, :, None, :]

            def step(hc, inp):
                dA_t, dBx_t, C_t = inp
                hc = dA_t * hc + dBx_t
                return (hc, jnp.einsum('bdn,bn->bd', hc, C_t))
            h0 = jnp.zeros((Bsz, Di, N), dtype=x.dtype)
            _, ys = jax.lax.scan(step, h0, (jnp.moveaxis(dA, 1, 0), jnp.moveaxis(dBx, 1, 0), jnp.moveaxis(Cm, 1, 0)))
            y = jnp.moveaxis(ys, 0, 1) + x * Dp
            y = y * _silu(z)
            return jnp.einsum('bld,ed->ble', y, W_out)
        out = _mamba_dir(hidden_states, W_in, conv_w_fwd, conv_b_fwd, Wx_fwd, Wdt_fwd, bdt_fwd, A_log_fwd, D_fwd, W_out)
        h_rev = jnp.flip(hidden_states, axis=-2)
        out_rev = _mamba_dir(h_rev, W_in, conv_w_rev, conv_b_rev, Wx_rev, Wdt_rev, bdt_rev, A_log_rev, D_rev, W_out)
        return out + jnp.flip(out_rev, axis=-2)

    def _L0_ffn_ref(x, weight, ln_gamma, ln_beta):
        import jax, jax.numpy as jnp
        import numpy as np
        LN_EPS = 0.001
        EPS = 1e-05
        QB = 128.0

        def ste_round(x):
            return x + jax.lax.stop_gradient(jnp.round(x) - x)
        mu = jnp.mean(x, axis=-1, keepdims=True)
        var = jnp.var(x, axis=-1, keepdims=True)
        xn = (x - mu) * jax.lax.rsqrt(var + LN_EPS) * ln_gamma + ln_beta
        beta = jnp.mean(jnp.abs(weight))
        w_q = jnp.clip(ste_round(weight / (beta + EPS)), -1.0, 1.0)
        gamma = jnp.max(jnp.abs(xn))
        xq = jnp.clip(xn * QB / gamma, -QB + EPS, QB - EPS)
        y = jnp.einsum('bsd,du->bsu', xq, w_q)
        return y * (gamma * beta / QB)
    x = L0_attn_hidden_states
    x = _layernorm(x + _L0_attn_ref(x, L0_attn_W_in, L0_attn_W_out, L0_attn_conv_w_fwd, L0_attn_conv_b_fwd, L0_attn_Wx_fwd, L0_attn_Wdt_fwd, L0_attn_bdt_fwd, L0_attn_A_log_fwd, L0_attn_D_fwd, L0_attn_conv_w_rev, L0_attn_conv_b_rev, L0_attn_Wx_rev, L0_attn_Wdt_rev, L0_attn_bdt_rev, L0_attn_A_log_rev, L0_attn_D_rev), axis=-1)
    x = _layernorm(x + _L0_ffn_ref(x, L0_ffn_weight, L0_ffn_ln_gamma, L0_ffn_ln_beta), axis=-1)
    return x

_drawn_inputs = setup_inputs


def setup_inputs(seed=0):
    import zlib

    import numpy as np

    out = dict(_drawn_inputs(seed))
    spreads = {'L0_attn_conv_b_fwd': (0.0, 0.8),
     'L0_attn_bdt_fwd': (-4.599999904632568, 0.6),
     'L0_attn_D_fwd': (1.0, 0.6),
     'L0_attn_conv_b_rev': (0.0, 0.8),
     'L0_attn_bdt_rev': (-4.599999904632568, 0.6),
     'L0_attn_D_rev': (1.0, 0.6),
     'L0_ffn_ln_gamma': (1.0, 0.2),
     'L0_ffn_ln_beta': (0.0, 0.512)}
    factors = {'L0_attn_W_in': 8.0,
     'L0_attn_W_out': 8.0,
     'L0_attn_conv_w_fwd': 8.0,
     'L0_attn_Wx_fwd': 8.0,
     'L0_attn_Wdt_fwd': 8.0,
     'L0_attn_A_log_fwd': 8.0,
     'L0_attn_conv_w_rev': 8.0,
     'L0_attn_Wx_rev': 8.0,
     'L0_attn_Wdt_rev': 8.0,
     'L0_attn_A_log_rev': 8.0}
    for name, (base, spread) in spreads.items():
        noise = np.random.default_rng([zlib.crc32(name.encode()), seed]).standard_normal(out[name].shape)
        drawn = base * np.exp(spread * noise) if base else spread * noise
        out[name] = jnp.asarray(drawn.astype(out[name].dtype))
    for name, factor in factors.items():
        out[name] = (out[name] * factor).astype(out[name].dtype)
    return out
```

```python
import concourse.bass as bass
from concourse import mybir
from contextlib import ExitStack

BATCH, SEQ, MODEL = 4, 1024, 128
INNER, STATES, TAPS, RANK = 256, 16, 4, 64
P = 128
DT = INNER // P
CHUNK = 512
CHUNKS = SEQ // CHUNK
TT = CHUNK // P
TILES = BATCH * SEQ // P
FWD, REV = 0, 1
GROUPS = ((FWD, 0), (FWD, 1), (REV, 1), (REV, 0))
NG = len(GROUPS)
RING = 4
LEAD = 3
POOL_C = (3, 8, 13)
NPC = len(POOL_C)
NVC = STATES - NPC
LN1_EPS, LN2_EPS, QUANT_EPS, QB = 1e-5, 1e-3, 1e-5, 128.0
ROUND = 1.5 * 2.0 ** 23
EXP_LN = "natural_log_exp_and_others"


def vector_c_before(n):
    return sum(m not in POOL_C for m in range(n))


def pool_c_before(n):
    return sum(m in POOL_C for m in range(n))


def build(nc, h, w_in, w_out, conv_w_f, conv_b_f, wx_f, wdt_f, bdt_f, alog_f, d_f,
          conv_w_r, conv_b_r, wx_r, wdt_r, bdt_r, alog_r, d_r, w_ffn, ln_gamma, ln_beta, out):
    f32, bf16 = mybir.dt.float32, mybir.dt.bfloat16
    ALU = mybir.AluOpType
    ACT = mybir.ActivationFunctionType
    X = mybir.AxisListType.X
    REDUCE = bass.bass_isa.ReduceOp

    h_tiles = h.rearrange("b (t p) m -> b p t m", p=P)
    out_tiles = out.rearrange("b (t p) m -> p (b t) m", p=P)

    with ExitStack() as ctx:
        def sb(name, shape, dt=f32):
            return ctx.enter_context(nc.sbuf_tensor(name, shape, dt))

        def pb(name, shape):
            return ctx.enter_context(nc.psum_tensor(name, shape, f32))

        def sem(name):
            return ctx.enter_context(nc.semaphore(name))

        ident = sb("ident", [P, P])
        select = sb("select", [P, 2 * STATES, P], bf16)
        w_in_t = sb("w_in_t", [P, 2 * INNER])
        w_mix_t = sb("w_mix_t", [P, 4, P])
        wx_rev_t = sb("wx_rev_t", [P, DT, P])
        wdt_t = sb("wdt_t", [P, 2, DT, P])
        diag_d = sb("diag_d", [P, 2, DT, P])
        conv_w = sb("conv_w", [P, 2, DT, TAPS])
        conv_b = sb("conv_b", [P, 2, DT])
        bdt = sb("bdt", [P, 2, DT])
        d_col = sb("d_col", [P, 2, DT])
        neg_a = sb("neg_a", [P, 2, DT, STATES])
        gamma_col = sb("gamma_col", [P, 1])
        beta_col = sb("beta_col", [P, 1])
        w_raw = sb("w_raw", [P, P])
        w_q = sb("w_q", [P, P])
        h_in = sb("h_in", [P, SEQ // P, P])
        h_res = sb("h_res", [P, SEQ // P, P])
        h_t = sb("h_t", [P, SEQ])
        PAD = TAPS - 1
        x_pad = sb("x_pad", [P, DT, PAD + SEQ + PAD])
        silu_z = sb("silu_z", [P, DT, SEQ])
        xs = sb("xs", [P, 2, DT, CHUNK])
        dt = sb("dt", [P, 2, DT, CHUNK])
        dtx = sb("dtx", [P, 2, DT, CHUNK])
        bc_parts = sb("bc_parts", [P, 2, CHUNK], bf16)
        x_dbl = sb("x_dbl", [P, CHUNK])
        bc_rest = sb("bc_rest", [64, CHUNK])
        sp_e = sb("sp_e", [P, DT, CHUNK])
        sp_s = sb("sp_s", [P, DT, CHUNK])
        above_one = sb("above_one", [P, 1])
        sp_r = sb("sp_r", [P, DT, CHUNK])
        sp_l = sb("sp_l", [P, DT, CHUNK])
        b_ring = sb("b_ring", [P, RING, CHUNK])
        c_ring = sb("c_ring", [P, NPC, CHUNK])
        dbx = sb("dbx", [P, RING, DT, CHUNK])
        hs = sb("hs", [P, RING, DT, CHUNK])
        ch = sb("ch", [P, RING, DT, CHUNK])
        carry = sb("carry", [P, DT, STATES])
        y_fwd = sb("y_fwd", [P, CHUNKS, DT, CHUNK])
        gated = sb("gated", [P, DT, CHUNK])
        resid = sb("resid", [P, TT, P])
        stats = sb("stats", [P, TT, 6])
        mv1 = sb("mv1", [P, TT, 2])
        mv2 = sb("mv2", [P, TT, 2])
        rstd1 = sb("rstd1", [P, TT])
        rstd2 = sb("rstd2", [P, TT])
        xn = sb("xn", [P, TT, P])
        x1 = sb("x1", [P, TILES, P])
        xn_t = sb("xn_t", [P, TILES * P])
        part_max = sb("part_max", [P, TILES // TT])
        half = sb("half", [P, TILES])
        tiny = sb("tiny", [P, 16])
        w_in_raw = ch[:, 0, :, :].rearrange("p a t -> p (a t)")[:, 0:4 * P].rearrange("p (q m) -> p q m", q=4)
        w_out_raw = ch[:, 1, 0, 0:INNER]
        wx_raw = ch[:, 1, 1, :].rearrange("p (g e) -> p g e", g=2)
        wdt_raw = ch[:, 2, 0, :].rearrange("p (g a r) -> p g a r", g=2, a=DT)
        z_last = hs[:, :, :, :].rearrange("p a b t -> p (a b t)").rearrange("p (j m) -> p j m", m=P)
        stats_last = ch[:, 0, 0, 0:TILES * 6].rearrange("p (j s) -> p j s", s=6)
        mv_last = ch[:, 0, 1, 0:TILES * 2].rearrange("p (j s) -> p j s", s=2)
        rstd_last = ch[:, 1, 0, 0:TILES]

        y_ps = pb("y_ps", [P, DT, CHUNK])
        da_ps = pb("da_ps", [P, DT, CHUNK])
        b_ps = pb("b_ps", [P, CHUNK])
        c_ps = pb("c_ps", [P, CHUNK])
        pre_a = pb("pre_a", [P, CHUNK])
        pre_b = pb("pre_b", [P, CHUNK])

        (weights_in, cols_in, ident_zero, ident_ready, pads_ready, raw_zero, half_ready, small_dve, select_sum, select_ready, weights_ps,
         weights_sb, a_exp, a_ready, diag_ready, h_in_ready, h_res_ready, ht_ps, ht_sb, x_ps, x_sb, z_ps,
         z_raw, silu_z_ready, tap0, conv, xs_ready, x_dbl_ps, x_dbl_sb, bc_hi, bc_rest_ready, bc_mid, bc_ready,
         u_ps, u_taken, sp_e_ready, sp_l_ready, sp_square, sp_cube, sp_min, dt_ready, dtx_ready,
         b_ps_ready, b_sb_ready, dbx_ready, da_ready, scanned, carried, c_ps_ready, c_sb_ready, ch_vector,
         ch_pool, summed, y_saved, y_added, g_ready, o_ps, resid_ready, stats_ready, mv1_ready,
         rstd1_ready, x1_ready, x1_kept, mv2_ready, rstd2_ready, xn_ready, xn_ps, xn_sb, max_ready, all_max,
         w_sum, w_sum_all, wq_ready, scaled, scale_ready, clipped, out_ps, z_ready, mv_last_ready,
         rstd_last_ready, final_ready, stored) = [sem(n) for n in (
             "weights_in cols_in ident_zero ident_ready pads_ready raw_zero half_ready small_dve select_sum select_ready weights_ps "
             "weights_sb a_exp a_ready diag_ready h_in_ready h_res_ready ht_ps ht_sb x_ps x_sb z_ps "
             "z_raw silu_z_ready tap0 conv xs_ready x_dbl_ps x_dbl_sb bc_hi bc_rest_ready bc_mid bc_ready "
             "u_ps u_taken sp_e_ready sp_l_ready sp_square sp_cube sp_min dt_ready dtx_ready "
             "b_ps_ready b_sb_ready dbx_ready da_ready scanned carried c_ps_ready c_sb_ready ch_vector "
             "ch_pool summed y_saved y_added g_ready o_ps resid_ready stats_ready mv1_ready "
             "rstd1_ready x1_ready x1_kept mv2_ready rstd2_ready xn_ready xn_ps xn_sb max_ready all_max "
             "w_sum w_sum_all wq_ready scaled scale_ready clipped out_ps z_ready mv_last_ready "
             "rstd_last_ready final_ready stored").split()]

        block = ctx.enter_context(nc.Block())

        def following(b, s):
            return (b, s + 1) if s + 1 < NG else (b + 1, 0)

        def batches(eng, body):
            body(0, True, False)
            with eng.Fori(1, BATCH - 1) as b:
                body(b, False, False)
            body(BATCH - 1, False, True)

        def wait_c_product(eng, b, s, n):
            group = NG * b + s
            if n in POOL_C:
                eng.wait_ge(ch_pool, NPC * group + pool_c_before(n) + 1)
            else:
                eng.wait_ge(ch_vector, NVC * group + vector_c_before(n) + 1)

        def chunk_of(s):
            c = GROUPS[s][1]
            return slice(c * CHUNK, (c + 1) * CHUNK)

        def in_scan_order(ap, s):
            return ap if GROUPS[s][0] == FWD else ap[:, ::-1]

        def last_column(s):
            return CHUNK - 1 if GROUPS[s][0] == FWD else 0

        @block.sync
        def _(sp):
            sp.dma_start(h_in[:], h_tiles[0]).then_inc(h_in_ready, 16)
            sp.dma_start(w_in_raw, w_in.rearrange("(q p) m -> p q m", p=P)).then_inc(weights_in, 16)
            for g, wx in enumerate((wx_f, wx_r)):
                sp.dma_start(wx_raw[0:32, g, :], wx[RANK:RANK + 32, :]).then_inc(weights_in, 16)
                sp.dma_start(wx_raw[32:64, g, :], wx[RANK:RANK + 32, :]).then_inc(weights_in, 16)
                sp.dma_start(wx_raw[64:128, g, :], wx[0:RANK, :]).then_inc(weights_in, 16)
            for g, wdt in enumerate((wdt_f, wdt_r)):
                sp.dma_start(wdt_raw[:, g, :, RANK:], wdt.rearrange("(a p) r -> p a r", p=P)).then_inc(weights_in, 16)
            sp.dma_start(w_out_raw, w_out).then_inc(weights_in, 16)
            for g, (cw, cb, bd, al, d) in enumerate(((conv_w_f, conv_b_f, bdt_f, alog_f, d_f),
                                                     (conv_w_r, conv_b_r, bdt_r, alog_r, d_r))):
                sp.dma_start(conv_w[:, g], cw.rearrange("(a p) k -> p a k", p=P)).then_inc(cols_in, 16)
                sp.dma_start(conv_b[:, g], cb.rearrange("(a p) -> p a", p=P), allow_slow_non_contiguous=True).then_inc(cols_in, 16)
                sp.dma_start(bdt[:, g], bd.rearrange("(a p) -> p a", p=P), allow_slow_non_contiguous=True).then_inc(cols_in, 16)
                sp.dma_start(neg_a[:, g], al.rearrange("(a p) n -> p a n", p=P)).then_inc(cols_in, 16)
                sp.dma_start(d_col[:, g], d.rearrange("(a p) -> p a", p=P), allow_slow_non_contiguous=True).then_inc(cols_in, 16)
            sp.dma_start(gamma_col[:], ln_gamma.rearrange("(p o) -> p o", o=1)).then_inc(cols_in, 16)
            sp.dma_start(beta_col[:], ln_beta.rearrange("(p o) -> p o", o=1)).then_inc(cols_in, 16)
            sp.dma_start(w_raw[:], w_ffn).then_inc(cols_in, 16)

            def batch(b, first, last):
                if not first:
                    sp.wait_ge(resid_ready, 2 * b)
                sp.dma_start(h_res[:], h_tiles[bass.ds(b, 1)].rearrange("o p t m -> p (o t) m")
                             if not isinstance(b, int) else h_tiles[b]).then_inc(h_res_ready, 16)
                if not last:
                    sp.wait_ge(ht_ps, 2 * b + 2)
                    sp.dma_start(h_in[:], h_tiles[bass.ds(b + 1, 1)].rearrange("o p t m -> p (o t) m")
                                 if not isinstance(b, int) else h_tiles[b + 1]).then_inc(h_in_ready, 16)

            batches(sp, batch)
            for c in range(BATCH):
                sp.wait_ge(final_ready, c + 1)
                tiles = slice(c * TILES // BATCH, (c + 1) * TILES // BATCH)
                sp.dma_start(out_tiles[:, tiles, :], z_last[:, tiles, :]).then_inc(stored, 16)
            sp.wait_ge(stored, 16 * BATCH)

        @block.gpsimd
        def _(pool):
            nc.gpsimd.memset(ident[:], 0.0).then_inc(ident_zero, 1)
            pool.wait_ge(ident_zero, 1)
            nc.gpsimd.affine_select(out=ident[:], in_=ident[:], compare_op=ALU.not_equal, fill=1.0, base=0,
                                    pattern=[[-1, P]], channel_multiplier=1).then_inc(ident_ready, 1)
            nc.gpsimd.memset(wdt_raw[:, :, :, 0:RANK], 0.0).then_inc(raw_zero, 1)
            nc.gpsimd.memset(x_pad[:, :, 0:PAD], 0.0).then_inc(pads_ready, 1)
            nc.gpsimd.memset(x_pad[:, :, PAD + SEQ:], 0.0).then_inc(pads_ready, 1)
            nc.gpsimd.memset(bc_parts[:], 0.0).then_inc(pads_ready, 1)
            nc.gpsimd.memset(above_one[:], 1.0 + 2.0 ** -23).then_inc(pads_ready, 1)
            nc.gpsimd.memset(half[:], -0.5).then_inc(half_ready, 1)
            pool.wait_ge(w_sum, 1)
            nc.gpsimd.partition_all_reduce(tiny[:, 1:2], tiny[:, 0:1], P, REDUCE.add).then_inc(w_sum_all, 1)

            def times_b(b, s, n):
                group = NG * b + s
                if n == 0:
                    pool.wait_ge(dtx_ready, group + 1)
                pool.wait_ge(b_sb_ready, STATES * group + n + 1)
                if not (isinstance(group, int) and group == 0 and n < RING):
                    pool.wait_ge(scanned, DT * (STATES * group + n - RING + 1))
                nc.gpsimd.tensor_tensor(dbx[:, n % RING], dtx[:, s % 2],
                                        b_ring[:, n % RING, :].unsqueeze(1).to_broadcast([P, DT, CHUNK]),
                                        ALU.mult).then_inc(dbx_ready, 1)

            def times_c(b, s, n):
                group = NG * b + s
                pool.wait_ge(scanned, DT * (STATES * group + n + 1))
                pool.wait_ge(c_sb_ready, NPC * group + pool_c_before(n) + 1)
                if not (isinstance(group, int) and group == 0 and n < RING):
                    pool.wait_ge(summed, STATES * group + n - RING + 1)
                nc.gpsimd.tensor_tensor(ch[:, n % RING], hs[:, n % RING],
                                        c_ring[:, pool_c_before(n), :].unsqueeze(1).to_broadcast([P, DT, CHUNK]),
                                        ALU.mult).then_inc(ch_pool, 1)

            def inverse_deviation(e, mv, mv_ready, rstd, rstd_ready, eps):
                pool.wait_ge(mv_ready, 2 * (e + 1))
                nc.gpsimd.tensor_tensor(rstd[:], mv[:, :, 1], half[:, 0:TT], ALU.pow).then_inc(rstd_ready, 1)

            def batch(b, first, last):
                for s in range(NG):
                    for n in range(STATES):
                        if n - 1 in POOL_C:
                            times_c(b, s, n - 1)
                        if n + 2 < STATES:
                            times_b(b, s, n + 2)
                        elif not (last and s == NG - 1):
                            times_b(*following(b, s), n + 2 - STATES)
                        if s == NG - 1 or (s == 0 and not first):
                            e = 2 * b if s else 2 * b - 1
                            if n == 7:
                                inverse_deviation(e, mv1, mv1_ready, rstd1, rstd1_ready, LN1_EPS)
                            if n == 10:
                                inverse_deviation(e, mv2, mv2_ready, rstd2, rstd2_ready, LN2_EPS)

            times_b(0, 0, 0)
            times_b(0, 0, 1)
            batches(pool, batch)
            e = 2 * BATCH - 1
            inverse_deviation(e, mv1, mv1_ready, rstd1, rstd1_ready, LN1_EPS)
            inverse_deviation(e, mv2, mv2_ready, rstd2, rstd2_ready, LN2_EPS)
            pool.wait_ge(max_ready, 2 * BATCH + 1)
            nc.gpsimd.partition_all_reduce(tiny[:, 5:6], tiny[:, 4:5], P, REDUCE.max).then_inc(all_max, 1)
            for c in range(BATCH):
                pool.wait_ge(mv_last_ready, 2 * (c + 1))
                t = slice(c * TILES // BATCH, (c + 1) * TILES // BATCH)
                nc.gpsimd.tensor_tensor(rstd_last[:, t], mv_last[:, t, 1], half[:, t],
                                        ALU.pow).then_inc(rstd_last_ready, 1)

        @block.scalar
        def _(act):
            nc.scalar.preload_act_table_set(EXP_LN)
            act.wait_ge(cols_in, 16 * 13)
            nc.scalar.activation(neg_a[:], neg_a[:], ACT.Exp).then_inc(a_exp, 1)
            act.wait_ge(weights_ps, 4)
            nc.scalar.copy(w_in_t[:], y_ps[:, 0, :]).then_inc(weights_sb, 1)
            nc.scalar.copy(w_mix_t[:].rearrange("p a m -> p (a m)"), y_ps[:, 1, :]).then_inc(weights_sb, 1)
            nc.scalar.copy(wx_rev_t[:].rearrange("p a m -> p (a m)"), da_ps[:, 0, 0:2 * P]).then_inc(weights_sb, 1)
            nc.scalar.copy(wdt_t[:].rearrange("p g a m -> p (g a m)"), da_ps[:, 1, :]).then_inc(weights_sb, 1)

            def copy_ht(b, c):
                act.wait_ge(ht_ps, CHUNKS * b + c + 1)
                nc.scalar.copy(h_t[:, c * CHUNK:(c + 1) * CHUNK], pre_b[:]).then_inc(ht_sb, 1)

            def copy_x(b, j):
                a, c = divmod(j, CHUNKS)
                if j == 0 and not (isinstance(b, int) and b == 0):
                    act.wait_ge(conv, 6 * NG * b)
                act.wait_ge(x_ps, DT * CHUNKS * b + j + 1)
                nc.scalar.copy(x_pad[:, a, PAD + c * CHUNK:PAD + (c + 1) * CHUNK], pre_b[:]).then_inc(x_sb, 1)

            def copy_z(b, j):
                a, c = divmod(j, CHUNKS)
                if j == 0 and not (isinstance(b, int) and b == 0):
                    act.wait_ge(g_ready, CHUNKS * b)
                act.wait_ge(z_ps, DT * CHUNKS * b + j + 1)
                nc.scalar.copy(silu_z[:, a, c * CHUNK:(c + 1) * CHUNK], pre_b[:]).then_inc(z_raw, 1)

            def prepare(b, s, n, silu_gate=None):
                q = NG * b + s
                g, c = GROUPS[s]
                par = s % 2
                zero = isinstance(q, int) and q == 0
                if n == 0:
                    act.wait_ge(x_sb, DT * CHUNKS * (b + 1))
                    if zero:
                        act.wait_ge(pads_ready, 4)
                    if not (isinstance(q, int) and q < 2):
                        act.wait_ge(summed, STATES * (q - 1))
                        act.wait_ge(dtx_ready, q - 1)
                    for a in range(DT):
                        at = c * CHUNK + (0 if g == FWD else 2 * PAD)
                        nc.scalar.activation(xs[:, par, a, :], x_pad[:, a, at:at + CHUNK], ACT.Identity,
                                             scale=conv_w[:, g, a, 0:1], bias=conv_b[:, g, a:a + 1]).then_inc(tap0, 1)
                if n == 3:
                    act.wait_ge(conv, 6 * (q + 1))
                    nc.scalar.activation(xs[:, par], xs[:, par], ACT.Silu).then_inc(xs_ready, 1)
                    if silu_gate is not None:
                        act.wait_ge(z_raw, DT * CHUNKS * (silu_gate + 1))
                        nc.scalar.activation(silu_z[:], silu_z[:], ACT.Silu).then_inc(silu_z_ready, 1)
                    nc.scalar.preload_act_table_set(EXP_LN)
                if n == 5:
                    act.wait_ge(x_dbl_ps, q + 1)
                    if not zero:
                        act.wait_ge(u_ps, 2 * q)
                        act.wait_ge(bc_rest_ready, q)
                    nc.scalar.copy(x_dbl[:], pre_a[:]).then_inc(x_dbl_sb, 1)
                    if not (isinstance(q, int) and q < 2):
                        act.wait_ge(c_ps_ready, STATES * (q - 1))
                    nc.scalar.copy(bc_parts[0:64, par], pre_a[0:64, :]).then_inc(bc_hi, 1)
                if n == 6:
                    act.wait_ge(bc_rest_ready, q + 1)
                    nc.scalar.copy(bc_parts[32:64, par], bc_rest[32:64, :]).then_inc(bc_mid, 1)
                if n in (7, 8):
                    a = n - 7
                    act.wait_ge(u_ps, 2 * q + a + 1)
                    if not zero and a == 0:
                        act.wait_ge(dt_ready, q)
                    nc.scalar.activation(sp_e[:, a], pre_a[:], ACT.Abs, bias=bdt[:, g, a:a + 1]).then_inc(u_taken, 1)
                    nc.scalar.activation(sp_r[:, a], pre_a[:], ACT.Relu, bias=bdt[:, g, a:a + 1]).then_inc(u_taken, 1)
                if n == 8:
                    act.wait_ge(u_taken, 4 * (q + 1))
                    nc.scalar.activation(sp_e[:], sp_e[:], ACT.Exp, scale=-1.0).then_inc(sp_e_ready, 1)
                if n == 9:
                    act.wait_ge(sp_e_ready, q + 1)
                    nc.scalar.activation(sp_l[:], sp_e[:], ACT.Ln, bias=above_one[:]).then_inc(sp_l_ready, 1)

            def copy_b(b, s, n):
                group = NG * b + s
                act.wait_ge(b_ps_ready, STATES * group + n + 1)
                if not (isinstance(group, int) and group == 0 and n < RING):
                    act.wait_ge(dbx_ready, STATES * group + n - RING + 1)
                nc.scalar.copy(b_ring[:, n % RING, :], b_ps[:]).then_inc(b_sb_ready, 1)

            def keep_x1(b_e, h_e):
                e = 2 * b_e + h_e
                act.wait_ge(x1_ready, TT * (e + 1))
                tile = (SEQ // P) * b_e + (1 - h_e) * TT
                dst = x1[:, tile:tile + TT, :] if isinstance(tile, int) else x1[:, bass.ds(tile, TT), :]
                nc.scalar.copy(dst, xn[:]).then_inc(x1_kept, 1)

            def norm_out(b_e, h_e):
                e = 2 * b_e + h_e
                act.wait_ge(xn_ps, e + 1)
                col = (SEQ * b_e + (1 - h_e) * CHUNK)
                dst = xn_t[:, col:col + CHUNK] if isinstance(col, int) else xn_t[:, bass.ds(col, CHUNK)]
                nc.scalar.activation(dst, pre_b[:], ACT.Identity,
                                     scale=gamma_col[:], bias=beta_col[:]).then_inc(xn_sb, 1)

            def batch(b, first, last):
                for s in range(NG):
                    group = NG * b + s
                    g, c = GROUPS[s]
                    if not first and s == 0:
                        nc.scalar.preload_act_table_set(EXP_LN)
                    for n in range(STATES):
                        if n + LEAD < STATES:
                            copy_b(b, s, n + LEAD)
                        elif not (last and s == NG - 1):
                            copy_b(*following(b, s), n + LEAD - STATES)
                        for a in range(DT):
                            if n == 0 and a == 0:
                                act.wait_ge(dt_ready, group + 1)
                            if not (isinstance(group, int) and group == 0 and n == 0):
                                act.wait_ge(scanned, DT * (STATES * group + n - 1) + a + 1)
                            nc.scalar.activation(da_ps[:, a, :], dt[:, s % 2, a, :], ACT.Exp,
                                                 scale=neg_a[:, g, a, n:n + 1]).then_inc(da_ready, 1)
                        if n == 2 and GROUPS[s - 1][0] == FWD and s > 0:
                            act.wait_ge(summed, STATES * group)
                            if not first:
                                act.wait_ge(y_added, CHUNKS * b)
                            nc.scalar.copy(y_fwd[:, GROUPS[s - 1][1]], y_ps[:]).then_inc(y_saved, 1)
                        if n in POOL_C:
                            act.wait_ge(c_ps_ready, STATES * group + n + 1)
                            if not (isinstance(group, int) and group == 0):
                                act.wait_ge(ch_pool, NPC * (group - 1) + pool_c_before(n) + 1)
                            nc.scalar.copy(c_ring[:, pool_c_before(n), :], c_ps[:]).then_inc(c_sb_ready, 1)
                        if not (last and s == NG - 1):
                            prepare(*following(b, s), n, silu_gate=b if s == 2 else None)
                        if s == 1 and n in (5, 6, 7, 8):
                            copy_z(b, n - 5)
                        if s == 2 and not last:
                            if n in (4, 5):
                                copy_ht(b + 1, n - 4)
                            if n in (6, 7, 8, 9):
                                copy_x(b + 1, n - 6)
                        if s == NG - 1 or (s == 0 and not first):
                            of, h_e = (b, 0) if s else (b - 1, 1)
                            if n == 9:
                                keep_x1(of, h_e)
                            if n == 13:
                                norm_out(of, h_e)

            copy_ht(0, 0)
            copy_ht(0, 1)
            for j in range(DT * CHUNKS):
                copy_x(0, j)
            for n in range(STATES):
                prepare(0, 0, n)
            for n in range(LEAD):
                copy_b(0, 0, n)
            batches(act, batch)
            keep_x1(BATCH - 1, 1)
            norm_out(BATCH - 1, 1)
            act.wait_ge(scale_ready, 1)
            for c in range(2 * BATCH):
                t = slice(c * CHUNK, (c + 1) * CHUNK)
                nc.scalar.activation(xn_t[:, t], xn_t[:, t], ACT.Copy, scale=tiny[:, 7:8]).then_inc(scaled, 1)

        @block.vector
        def _(dve):
            small = [0]

            def chained(ins):
                small[0] += 1
                ins.then_inc(small_dve, 1)
                dve.wait_ge(small_dve, small[0])

            dve.wait_ge(ident_ready, 1)
            chained(nc.vector.tensor_tensor(xn[:, 0, 0:32], ident[:, 0:32], ident[:, 32:64], ALU.add))
            chained(nc.vector.tensor_tensor(xn[:, 0, 0:32], xn[:, 0, 0:32], ident[:, 64:96], ALU.add))
            nc.vector.tensor_copy(select[:], xn[:, 0, 0:32].unsqueeze(2).to_broadcast([P, 2 * STATES, P])
                                  ).then_inc(select_ready, 1)
            dve.wait_ge(a_exp, 1)
            nc.vector.tensor_scalar(neg_a[:], neg_a[:], -1.0, None, ALU.mult).then_inc(a_ready, 1)
            for g in range(2):
                for a in range(DT):
                    nc.vector.tensor_scalar(diag_d[:, g, a, :], ident[:], d_col[:, g, a:a + 1], None,
                                            ALU.mult).then_inc(diag_ready, 1)
            nc.vector.tensor_reduce(tiny[:, 0:1], w_raw[:], X, ALU.add, apply_absolute_value=True).then_inc(w_sum, 1)

            def quantise_weight():
                dve.wait_ge(w_sum_all, 1)
                chained(nc.vector.tensor_scalar(tiny[:, 2:3], tiny[:, 1:2], 1.0 / (P * P), None, ALU.mult))
                chained(nc.vector.tensor_scalar(tiny[:, 3:4], tiny[:, 2:3], QUANT_EPS, None, ALU.add))
                chained(nc.vector.reciprocal(tiny[:, 3:4], tiny[:, 3:4]))
                chained(nc.vector.tensor_scalar(w_q[:], w_raw[:], tiny[:, 3:4], ROUND, ALU.mult, ALU.add))
                chained(nc.vector.tensor_scalar(w_q[:], w_q[:], ROUND, 1.0, ALU.subtract, ALU.min))
                nc.vector.tensor_scalar(w_q[:], w_q[:], -1.0, None, ALU.max).then_inc(wq_ready, 1)

            def prepare(b, s, n):
                q = NG * b + s
                g, c = GROUPS[s]
                par = s % 2
                if n in (0, 1, 2):
                    k = n + 1
                    for a in range(DT):
                        if k == 1:
                            dve.wait_ge(tap0, DT * q + a + 1)
                        else:
                            dve.wait_ge(conv, 6 * q + DT * (k - 2) + a + 1)
                        at = c * CHUNK + (k if g == FWD else 2 * PAD - k)
                        nc.vector.scalar_tensor_tensor(xs[:, par, a, :], x_pad[:, a, at:at + CHUNK],
                                                       conv_w[:, g, a, k:k + 1], xs[:, par, a, :],
                                                       ALU.mult, ALU.add).then_inc(conv, 1)
                if n == 5:
                    dve.wait_ge(x_dbl_sb, q + 1)
                    dve.wait_ge(bc_hi, q + 1)
                    nc.vector.tensor_tensor(bc_rest[:], x_dbl[0:64, :], bc_parts[0:64, par],
                                            ALU.subtract).then_inc(bc_rest_ready, 1)
                if n == 6:
                    dve.wait_ge(bc_mid, q + 1)
                    nc.vector.tensor_tensor(bc_parts[64:96, par], bc_rest[32:64, :], bc_parts[32:64, par],
                                            ALU.subtract).then_inc(bc_ready, 1)
                if n == 9:
                    dve.wait_ge(sp_e_ready, q + 1)
                    nc.vector.scalar_tensor_tensor(sp_s[:], sp_e[:], 1.5, sp_e[:],
                                                   ALU.subtract, ALU.mult).then_inc(sp_square, 1)
                if n == 10:
                    dve.wait_ge(sp_square, q + 1)
                    nc.vector.scalar_tensor_tensor(sp_s[:], sp_s[:], 3.0, sp_e[:],
                                                   ALU.add, ALU.mult).then_inc(sp_cube, 1)
                if n == 11:
                    dve.wait_ge(sp_cube, q + 1)
                    dve.wait_ge(sp_l_ready, q + 1)
                    nc.vector.scalar_tensor_tensor(sp_s[:], sp_l[:], 3.0, sp_s[:],
                                                   ALU.mult, ALU.min).then_inc(sp_min, 1)
                    dve.wait_ge(sp_min, q + 1)
                    if not (isinstance(q, int) and q < 2):
                        dve.wait_ge(da_ready, DT * STATES * (q - 1))
                    nc.vector.scalar_tensor_tensor(dt[:, par], sp_s[:], 1.0 / 3.0, sp_r[:],
                                                   ALU.mult, ALU.add).then_inc(dt_ready, 1)
                if n == 12:
                    dve.wait_ge(dt_ready, q + 1)
                    dve.wait_ge(xs_ready, q + 1)
                    if not (isinstance(q, int) and q < 2):
                        dve.wait_ge(dbx_ready, STATES * (q - 1))
                    nc.vector.tensor_tensor(dtx[:, par], dt[:, par], xs[:, par], ALU.mult).then_inc(dtx_ready, 1)

            def times_c(b, s, n):
                group = NG * b + s
                dve.wait_ge(c_ps_ready, STATES * group + n + 1)
                dve.wait_ge(scanned, DT * (STATES * group + n + 1))
                if not (isinstance(group, int) and group == 0 and n < RING):
                    dve.wait_ge(summed, STATES * group + n - RING + 1)
                nc.vector.tensor_tensor(ch[:, n % RING], hs[:, n % RING],
                                        c_ps[:].unsqueeze(1).to_broadcast([P, DT, CHUNK]),
                                        ALU.mult).then_inc(ch_vector, 1)

            def keep_state(b, s, n):
                dve.wait_ge(scanned, DT * (STATES * (NG * b + s) + n + 1))
                nc.vector.tensor_copy(carry[:, :, n:n + 1],
                                      hs[:, n % RING, :, last_column(s):last_column(s) + 1]).then_inc(carried, 1)

            def add_directions(b, s):
                group = NG * b + s
                dve.wait_ge(summed, STATES * (group + 1))
                dve.wait_ge(y_saved, CHUNKS * (b + 1))
                c = GROUPS[s][1]
                nc.vector.tensor_tensor(y_fwd[:, c], y_ps[:], y_fwd[:, c], ALU.add).then_inc(y_added, 1)

            def gate(b, s):
                c = GROUPS[s][1]
                e = 2 * b + (1 if s == 3 else 0)
                dve.wait_ge(y_added, e + 1)
                dve.wait_ge(silu_z_ready, b + 1)
                if not (isinstance(e, int) and e == 0):
                    dve.wait_ge(o_ps, e)
                nc.vector.tensor_tensor(gated[:], y_fwd[:, c], silu_z[:, :, chunk_of(s)],
                                        ALU.mult).then_inc(g_ready, 1)

            def statistics(source, e, layer):
                for j in range(TT):
                    nc.vector.bn_stats(stats[:, j, :], source[:, j, :]).then_inc(stats_ready, 1)

            def statistics_wait(e, layer):
                dve.wait_ge(stats_ready, 2 * TT * e + TT * (layer + 1))

            def aggregate(e, layer):
                mv, mv_ready, eps = ((mv1, mv1_ready, LN1_EPS), (mv2, mv2_ready, LN2_EPS))[layer]
                for j in range(TT):
                    ins = nc.vector.bn_aggr(mv[:, j, :], stats[:, j, :])
                ins.then_inc(mv_ready, 1)
                dve.wait_ge(mv_ready, 2 * e + 1)
                nc.vector.tensor_scalar(mv[:, :, 1], mv[:, :, 1], eps, None, ALU.add).then_inc(mv_ready, 1)

            def norm_step(b, h_e, n):
                e = 2 * b + h_e
                tile0 = (1 - h_e) * TT
                if n == 5:
                    dve.wait_ge(h_res_ready, 16 * (b + 1))
                    dve.wait_ge(o_ps, e + 1)
                    nc.vector.tensor_tensor(resid[:], pre_b[:].rearrange("p (t m) -> p t m", t=TT),
                                            h_res[:, tile0:tile0 + TT, :], ALU.add).then_inc(resid_ready, 1)
                    dve.wait_ge(resid_ready, e + 1)
                    statistics(resid, e, 0)
                if n == 6:
                    aggregate(e, 0)
                if n == 8:
                    dve.wait_ge(rstd1_ready, e + 1)
                    for j in range(TT):
                        nc.vector.tensor_scalar(xn[:, j, :], resid[:, j, :], mv1[:, j, 0:1], rstd1[:, j:j + 1],
                                                ALU.subtract, ALU.mult).then_inc(x1_ready, 1)
                    dve.wait_ge(x1_ready, TT * (e + 1))
                    statistics(xn, e, 1)
                if n == 9:
                    aggregate(e, 1)
                if n == 11:
                    dve.wait_ge(x1_kept, e + 1)
                    dve.wait_ge(rstd2_ready, e + 1)
                    for j in range(TT):
                        nc.vector.tensor_scalar(xn[:, j, :], xn[:, j, :], mv2[:, j, 0:1], rstd2[:, j:j + 1],
                                                ALU.subtract, ALU.mult).then_inc(xn_ready, 1)
                if n == 14:
                    dve.wait_ge(xn_sb, e + 1)
                    col = SEQ * b + (1 - h_e) * CHUNK
                    slot = part_max[:, e:e + 1] if isinstance(e, int) else part_max[:, bass.ds(e, 1)]
                    src = xn_t[:, col:col + CHUNK] if isinstance(col, int) else xn_t[:, bass.ds(col, CHUNK)]
                    nc.vector.tensor_reduce(slot, src, X, ALU.max, apply_absolute_value=True).then_inc(max_ready, 1)

            def batch(b, first, last):
                for s in range(NG):
                    group = NG * b + s
                    g, c = GROUPS[s]
                    starts = s in (0, 2)
                    for n in range(STATES):
                        if n in (6, 9):
                            if s == NG - 1:
                                statistics_wait(2 * b, n // 9)
                            if s == 0 and not first:
                                statistics_wait(2 * b - 1, n // 9)
                        for a in range(DT):
                            idx = STATES * group + n
                            dve.wait_ge(da_ready, DT * idx + a + 1)
                            if a == 0:
                                dve.wait_ge(dbx_ready, idx + 1)
                                if n >= RING:
                                    wait_c_product(dve, b, s, n - RING)
                                elif not (first and s == 0):
                                    pb_, ps_ = (b, s - 1) if s else (b - 1, NG - 1)
                                    wait_c_product(dve, pb_, ps_, n - RING + STATES)
                            if starts:
                                initial = 0.0
                            else:
                                initial = carry[:, a, n:n + 1]
                                if n == 0 and a == 0:
                                    dve.wait_ge(carried, STATES * (2 * b + s // 2) + 1)
                                elif a == 0:
                                    dve.wait_ge(carried, STATES * (2 * b + s // 2) + n + 1)
                            nc.vector.tensor_tensor_scan(in_scan_order(hs[:, n % RING, a, :], s),
                                                         in_scan_order(da_ps[:, a, :], s),
                                                         in_scan_order(dbx[:, n % RING, a, :], s),
                                                         initial, ALU.mult, ALU.add).then_inc(scanned, 1)
                        if n:
                            prev = (b, s, n - 1)
                        else:
                            prev = (b, s - 1, STATES - 1) if s else (b - 1, NG - 1, STATES - 1)
                        if n == 2 and s == 3:
                            add_directions(b, 2)
                        if n == 2 and s == 0 and not first:
                            add_directions(b - 1, 3)
                        if not (first and s == 0 and n == 0):
                            if prev[1] in (0, 2):
                                keep_state(*prev)
                            if prev[2] not in POOL_C:
                                times_c(*prev)
                        if n == 3 and s == 3:
                            gate(b, 2)
                        if n == 3 and s == 0 and not first:
                            gate(b - 1, 3)
                        if not (last and s == NG - 1):
                            prepare(*following(b, s), n)
                        if s == NG - 1:
                            norm_step(b, 0, n)
                        if s == 0 and not first:
                            norm_step(b - 1, 1, n)
                        if first and s == 1 and n == 4:
                            quantise_weight()

            for n in range(STATES):
                prepare(0, 0, n)
            batches(dve, batch)
            times_c(BATCH - 1, NG - 1, STATES - 1)
            add_directions(BATCH - 1, 3)
            gate(BATCH - 1, 3)
            for n in range(STATES):
                if n in (6, 9):
                    statistics_wait(2 * BATCH - 1, n // 9)
                norm_step(BATCH - 1, 1, n)
            dve.wait_ge(max_ready, 2 * BATCH)
            nc.vector.tensor_reduce(tiny[:, 4:5], part_max[:], X, ALU.max).then_inc(max_ready, 1)
            dve.wait_ge(all_max, 1)
            chained(nc.vector.reciprocal(tiny[:, 6:7], tiny[:, 5:6]))
            nc.vector.tensor_scalar(tiny[:, 7:8], tiny[:, 6:7], QB, None, ALU.mult).then_inc(scale_ready, 1)
            chained(nc.vector.tensor_scalar(tiny[:, 8:9], tiny[:, 5:6], tiny[:, 2:3], 1.0 / QB, ALU.mult, ALU.mult))

            def last_norm(c):
                per = TILES // BATCH
                t0 = c * per
                for i in range(2):
                    j = 2 * c + i
                    dve.wait_ge(out_ps, j + 1)
                    t = slice(j * TT, (j + 1) * TT)
                    bank = (pre_a, pre_b)[j % 2]
                    nc.vector.scalar_tensor_tensor(z_last[:, t, :].rearrange("p t m -> p (t m)"), bank[:],
                                                   tiny[:, 8:9], x1[:, t, :].rearrange("p t m -> p (t m)"),
                                                   ALU.mult, ALU.add).then_inc(z_ready, 1)
                    dve.wait_ge(z_ready, j + 1)
                    for m in range(TT):
                        nc.vector.bn_stats(stats_last[:, j * TT + m, :], z_last[:, j * TT + m, :]).then_inc(stats_ready, 1)
                dve.wait_ge(stats_ready, 2 * TT * 2 * BATCH + per * (c + 1))
                for m in range(per):
                    ins = nc.vector.bn_aggr(mv_last[:, t0 + m, :], stats_last[:, t0 + m, :])
                ins.then_inc(mv_last_ready, 1)
                dve.wait_ge(mv_last_ready, 2 * c + 1)
                nc.vector.tensor_scalar(mv_last[:, t0:t0 + per, 1], mv_last[:, t0:t0 + per, 1], LN1_EPS, None,
                                        ALU.add).then_inc(mv_last_ready, 1)
                dve.wait_ge(rstd_last_ready, c + 1)
                for m in range(t0, t0 + per):
                    ins = nc.vector.tensor_scalar(z_last[:, m, :], z_last[:, m, :], mv_last[:, m, 0:1],
                                                  rstd_last[:, m:m + 1], ALU.subtract, ALU.mult)
                ins.then_inc(final_ready, 1)

            def clip(c):
                dve.wait_ge(scaled, c + 1)
                t = slice(c * CHUNK, (c + 1) * CHUNK)
                nc.vector.tensor_scalar(xn_t[:, t], xn_t[:, t], QB - QUANT_EPS, -QB + QUANT_EPS,
                                        ALU.min, ALU.max).then_inc(clipped, 1)

            clip(0)
            clip(1)
            for c in range(BATCH):
                if c + 1 < BATCH:
                    clip(2 * c + 2)
                    clip(2 * c + 3)
                last_norm(c)

        @block.tensor
        def _(pe):
            pe.wait_ge(ident_ready, 1)
            pe.wait_ge(raw_zero, 1)
            pe.wait_ge(weights_in, 16 * 10)
            for q in range(4):
                ins = nc.tensor.transpose(y_ps[:, 0, q * P:(q + 1) * P], w_in_raw[:, q, :], ident[:])
            ins.then_inc(weights_ps, 1)
            for a in range(DT):
                nc.tensor.transpose(y_ps[:, 1, a * P:(a + 1) * P], w_out_raw[:, a * P:(a + 1) * P], ident[:])
                ins = nc.tensor.transpose(y_ps[:, 1, (2 + a) * P:(3 + a) * P], wx_raw[:, 0, a * P:(a + 1) * P], ident[:])
            ins.then_inc(weights_ps, 1)
            for a in range(DT):
                ins = nc.tensor.transpose(da_ps[:, 0, a * P:(a + 1) * P], wx_raw[:, 1, a * P:(a + 1) * P], ident[:])
            ins.then_inc(weights_ps, 1)
            for g in range(2):
                for a in range(DT):
                    k = DT * g + a
                    ins = nc.tensor.transpose(da_ps[:, 1, k * P:(k + 1) * P], wdt_raw[:, g, a, :], ident[:])
            ins.then_inc(weights_ps, 1)

            def wx_half(g, a):
                return w_mix_t[:, 2 + a, :] if g == FWD else wx_rev_t[:, a, :]

            def transpose_h(b, c):
                if c == 0:
                    pe.wait_ge(h_in_ready, 16 * (b + 1))
                    if not (isinstance(b, int) and b == 0):
                        pe.wait_ge(z_raw, DT * CHUNKS * b)
                else:
                    pe.wait_ge(ht_sb, CHUNKS * b + c)
                for t in range(TT):
                    ins = nc.tensor.transpose(pre_b[:, t * P:(t + 1) * P], h_in[:, c * TT + t, :], ident[:])
                ins.then_inc(ht_ps, 1)

            def project_x(b, j):
                a, c = divmod(j, CHUNKS)
                if j == 0:
                    pe.wait_ge(ht_sb, CHUNKS * (b + 1))
                else:
                    pe.wait_ge(x_sb, DT * CHUNKS * b + j)
                nc.tensor.matmul(pre_b[:], w_in_t[:, a * P:(a + 1) * P], h_t[:, c * CHUNK:(c + 1) * CHUNK],
                                 start=True, stop=True).then_inc(x_ps, 1)

            def project_z(b, j, first):
                a, c = divmod(j, CHUNKS)
                if j == 0 and first:
                    pe.wait_ge(x_sb, DT * CHUNKS)
                elif j == 0:
                    pe.wait_ge(xn_sb, 2 * b)
                else:
                    pe.wait_ge(z_raw, DT * CHUNKS * b + j)
                nc.tensor.matmul(pre_b[:], w_in_t[:, INNER + a * P:INNER + (a + 1) * P],
                                 h_t[:, c * CHUNK:(c + 1) * CHUNK], start=True, stop=True).then_inc(z_ps, 1)

            def prepare(b, s, n):
                q = NG * b + s
                g, c = GROUPS[s]
                par = s % 2
                if n == 4:
                    pe.wait_ge(xs_ready, q + 1)
                    if not (isinstance(q, int) and q == 0):
                        pe.wait_ge(u_taken, 4 * q)
                    for a in range(DT):
                        ins = nc.tensor.matmul(pre_a[:], wx_half(g, a), xs[:, par, a, :], start=a == 0, stop=a == DT - 1)
                    ins.then_inc(x_dbl_ps, 1)
                if n in (6, 7):
                    a = n - 6
                    if a == 0:
                        pe.wait_ge(x_dbl_sb, q + 1)
                        pe.wait_ge(bc_hi, q + 1)
                    else:
                        pe.wait_ge(u_taken, 4 * q + 2)
                    nc.tensor.matmul(pre_a[:], wdt_t[:, g, a, :], x_dbl[:], start=True, stop=True).then_inc(u_ps, 1)

            def broadcast_b(b, s, n):
                group = NG * b + s
                if n == 0:
                    pe.wait_ge(bc_ready, group + 1)
                if not (isinstance(group, int) and group == 0 and n == 0):
                    pe.wait_ge(b_sb_ready, STATES * group + n)
                nc.tensor.matmul(b_ps[:], select[:, n, :], bc_parts[:, s % 2], start=True, stop=True).then_inc(b_ps_ready, 1)

            def broadcast_c(b, s, n, first):
                group = NG * b + s
                if n and (n - 1) in POOL_C:
                    pe.wait_ge(c_sb_ready, NPC * group + pool_c_before(n))
                elif n or not (first and s == 0):
                    pe.wait_ge(ch_vector, NVC * group + vector_c_before(n))
                nc.tensor.matmul(c_ps[:], select[:, STATES + n, :], bc_parts[:, s % 2], start=True, stop=True).then_inc(c_ps_ready, 1)

            def add_state(b, s, n):
                wait_c_product(pe, b, s, n)
                for a in range(DT):
                    ins = nc.tensor.matmul(y_ps[:, a, :], ident[:], ch[:, n % RING, a, :], start=False, stop=n == STATES - 1)
                ins.then_inc(summed, 1)

            def start_sum(b, s, first):
                g, c = GROUPS[s]
                if s == 1 or s == 2:
                    pe.wait_ge(y_saved, CHUNKS * b + s)
                elif s == 3:
                    pe.wait_ge(y_added, CHUNKS * b + 1)
                elif not first:
                    pe.wait_ge(y_added, CHUNKS * b)
                else:
                    pe.wait_ge(weights_sb, 2)
                    pe.wait_ge(diag_ready, 4)
                for a in range(DT):
                    nc.tensor.matmul(y_ps[:, a, :], diag_d[:, g, a, :], xs[:, s % 2, a, :], start=True, stop=False)

            def output_product(b, h_e, last):
                e = 2 * b + h_e
                pe.wait_ge(g_ready, e + 1)
                if h_e == 0 and not last:
                    pe.wait_ge(x_sb, DT * CHUNKS * (b + 2))
                elif h_e == 0:
                    pe.wait_ge(z_raw, DT * CHUNKS * (b + 1))
                else:
                    pe.wait_ge(xn_sb, e)
                for t in range(TT):
                    for a in range(DT):
                        ins = nc.tensor.matmul(pre_b[:, t * P:(t + 1) * P], gated[:, a, t * P:(t + 1) * P],
                                               w_mix_t[:, a, :], start=a == 0, stop=a == DT - 1)
                ins.then_inc(o_ps, 1)

            def transpose_norm(b, h_e):
                e = 2 * b + h_e
                pe.wait_ge(xn_ready, TT * (e + 1))
                pe.wait_ge(resid_ready, e + 1)
                for t in range(TT):
                    ins = nc.tensor.transpose(pre_b[:, t * P:(t + 1) * P], xn[:, t, :], ident[:])
                ins.then_inc(xn_ps, 1)

            def batch(b, first, last):
                for s in range(NG):
                    for n in range(STATES):
                        if n + LEAD < STATES:
                            broadcast_b(b, s, n + LEAD)
                        elif not (last and s == NG - 1):
                            broadcast_b(*following(b, s), n + LEAD - STATES)
                        if n == 2:
                            start_sum(b, s, first)
                        if n >= 2:
                            add_state(b, s, n - 2)
                        elif s:
                            add_state(b, s - 1, n - 2 + STATES)
                        elif not first:
                            add_state(b - 1, NG - 1, n - 2 + STATES)
                        broadcast_c(b, s, n, first)
                        if not (last and s == NG - 1):
                            prepare(*following(b, s), n)
                        if s == 0 and not first:
                            if n == 4:
                                output_product(b - 1, 1, False)
                            if n == 12:
                                transpose_norm(b - 1, 1)
                        if s == 1 and n in (4, 5, 6, 7):
                            project_z(b, n - 4, first)
                        if s == 2 and not last:
                            if n in (3, 4):
                                transpose_h(b + 1, n - 3)
                            if n in (5, 6, 7, 8):
                                project_x(b + 1, n - 5)
                        if s == NG - 1:
                            if n == 4:
                                output_product(b, 0, last)
                            if n == 12:
                                transpose_norm(b, 0)

            transpose_h(0, 0)
            transpose_h(0, 1)
            pe.wait_ge(weights_sb, 4)
            for j in range(DT * CHUNKS):
                project_x(0, j)
            for n in range(STATES):
                prepare(0, 0, n)
            pe.wait_ge(select_ready, 1)
            for n in range(LEAD):
                broadcast_b(0, 0, n)
            batches(pe, batch)
            add_state(BATCH - 1, NG - 1, STATES - 2)
            add_state(BATCH - 1, NG - 1, STATES - 1)
            output_product(BATCH - 1, 1, True)
            transpose_norm(BATCH - 1, 1)
            pe.wait_ge(wq_ready, 1)
            for j in range(2 * BATCH):
                pe.wait_ge(clipped, j + 1)
                if j >= 2:
                    pe.wait_ge(z_ready, j - 1)
                else:
                    pe.wait_ge(xn_sb, 2 * BATCH)
                bank = (pre_a, pre_b)[j % 2]
                for t in range(TT):
                    k = (j * TT + t) * P
                    ins = nc.tensor.matmul(bank[:, t * P:(t + 1) * P], xn_t[:, k:k + P], w_q[:], start=True, stop=True)
                ins.then_inc(out_ps, 1)


_NAMES = ["L0_attn_hidden_states", "L0_attn_W_in", "L0_attn_W_out", "L0_attn_conv_w_fwd", "L0_attn_conv_b_fwd",
          "L0_attn_Wx_fwd", "L0_attn_Wdt_fwd", "L0_attn_bdt_fwd", "L0_attn_A_log_fwd", "L0_attn_D_fwd",
          "L0_attn_conv_w_rev", "L0_attn_conv_b_rev", "L0_attn_Wx_rev", "L0_attn_Wdt_rev", "L0_attn_bdt_rev",
          "L0_attn_A_log_rev", "L0_attn_D_rev", "L0_ffn_weight", "L0_ffn_ln_gamma", "L0_ffn_ln_beta"]


def kernel(**inputs):
    import numpy as np
    import concourse.bacc as bacc
    from concourse.bass_utils import run_bass_kernel_spmd

    nc = bacc.Bacc("TRN2", target_bir_lowering=False, num_devices=1)
    arrays, args = {}, []
    for name in _NAMES:
        a = np.ascontiguousarray(inputs[name])
        arrays[f"in_{name}"] = a
        args.append(nc.dram_tensor(f"in_{name}", a.shape, mybir.dt.from_np(a.dtype), kind="ExternalInput").ap())
    args.append(nc.dram_tensor("out", (BATCH, SEQ, MODEL), mybir.dt.float32, kind="ExternalOutput").ap())
    build(nc, *args)
    r = run_bass_kernel_spmd(nc, [arrays], core_ids=[0])
    return r.results[0]["out"]
```

```python
import concourse.bass as bass
from concourse import mybir
from contextlib import ExitStack

BATCH, SEQ, MODEL = 4, 1024, 128
INNER, STATES, TAPS, RANK = 256, 16, 4, 64
P = 128
DT = INNER // P
CHUNK = 512
CHUNKS = SEQ // CHUNK
TT = CHUNK // P
TILES = BATCH * SEQ // P
FWD, REV = 0, 1
GROUPS = ((FWD, 0), (FWD, 1), (REV, 1), (REV, 0))
NG = len(GROUPS)
RING = 4
LEAD = 3
POOL_C = (2, 6, 10, 14)
NPC = len(POOL_C)
NVC = STATES - NPC
LN1_EPS, LN2_EPS, QUANT_EPS, QB = 1e-5, 1e-3, 1e-5, 128.0
ROUND = 1.5 * 2.0 ** 23
EXP_LN = "natural_log_exp_and_others"


def vector_c_before(n):
    return sum(m not in POOL_C for m in range(n))


def pool_c_before(n):
    return sum(m in POOL_C for m in range(n))


def build(nc, h, w_in, w_out, conv_w_f, conv_b_f, wx_f, wdt_f, bdt_f, alog_f, d_f,
          conv_w_r, conv_b_r, wx_r, wdt_r, bdt_r, alog_r, d_r, w_ffn, ln_gamma, ln_beta, out):
    f32, bf16 = mybir.dt.float32, mybir.dt.bfloat16
    ALU = mybir.AluOpType
    ACT = mybir.ActivationFunctionType
    X = mybir.AxisListType.X
    REDUCE = bass.bass_isa.ReduceOp

    h_tiles = h.rearrange("b (t p) m -> b p t m", p=P)
    out_tiles = out.rearrange("b (t p) m -> p (b t) m", p=P)

    with ExitStack() as ctx:
        def sb(name, shape, dt=f32):
            return ctx.enter_context(nc.sbuf_tensor(name, shape, dt))

        def pb(name, shape):
            return ctx.enter_context(nc.psum_tensor(name, shape, f32))

        def sem(name):
            return ctx.enter_context(nc.semaphore(name))

        ident = sb("ident", [P, P])
        select = sb("select", [P, 2 * STATES, P], bf16)
        w_in_t = sb("w_in_t", [P, 2 * INNER])
        w_mix_t = sb("w_mix_t", [P, 4, P])
        wx_rev_t = sb("wx_rev_t", [P, DT, P])
        wdt_t = sb("wdt_t", [P, 2, DT, P])
        diag_d = sb("diag_d", [P, 2, DT, P])
        conv_w = sb("conv_w", [P, 2, DT, TAPS])
        conv_b = sb("conv_b", [P, 2, DT])
        bdt = sb("bdt", [P, 2, DT])
        d_col = sb("d_col", [P, 2, DT])
        neg_a = sb("neg_a", [P, 2, DT, STATES])
        gamma_col = sb("gamma_col", [P, 1])
        beta_col = sb("beta_col", [P, 1])
        w_raw = sb("w_raw", [P, P])
        w_q = sb("w_q", [P, P])
        h_in = sb("h_in", [P, SEQ // P, P])
        h_res = sb("h_res", [P, SEQ // P, P])
        h_t = sb("h_t", [P, SEQ])
        PAD = TAPS - 1
        x_pad = sb("x_pad", [P, DT, PAD + SEQ + PAD])
        silu_z = sb("silu_z", [P, DT, SEQ])
        xs = sb("xs", [P, 2, DT, CHUNK])
        dt = sb("dt", [P, 2, DT, CHUNK])
        dtx = sb("dtx", [P, 2, DT, CHUNK])
        bc_parts = sb("bc_parts", [P, 2, CHUNK], bf16)
        x_dbl = sb("x_dbl", [P, CHUNK])
        bc_rest = sb("bc_rest", [64, CHUNK])
        sp_e = sb("sp_e", [P, DT, CHUNK])
        sp_s = sb("sp_s", [P, DT, CHUNK])
        above_one = sb("above_one", [P, 1])
        minus_three_quarters = sb("minus_three_quarters", [P, 1])
        sp_r = sb("sp_r", [P, DT, CHUNK])
        sp_l = sb("sp_l", [P, DT, CHUNK])
        b_ring = sb("b_ring", [P, RING, CHUNK])
        c_ring = sb("c_ring", [P, NPC, CHUNK])
        dbx = sb("dbx", [P, RING, DT, CHUNK])
        hs = sb("hs", [P, RING, DT, CHUNK])
        ch = sb("ch", [P, RING, DT, CHUNK])
        carry = sb("carry", [P, DT, STATES])
        y_fwd = sb("y_fwd", [P, DT, CHUNK])
        gated = sb("gated", [P, DT, CHUNK])
        resid = sb("resid", [P, TT, P])
        stats = sb("stats", [P, TT, 6])
        mv1 = sb("mv1", [P, TT, 2])
        mv2 = sb("mv2", [P, TT, 2])
        rstd1 = sb("rstd1", [P, TT])
        rstd2 = sb("rstd2", [P, TT])
        xn = sb("xn", [P, TT, P])
        x1 = sb("x1", [P, TILES, P])
        xn_t = sb("xn_t", [P, TILES * P])
        part_max = sb("part_max", [P, TILES // TT])
        half = sb("half", [P, TILES])
        tiny = sb("tiny", [P, 16])
        w_in_raw = ch[:, 0, :, :].rearrange("p a t -> p (a t)")[:, 0:4 * P].rearrange("p (q m) -> p q m", q=4)
        w_out_raw = ch[:, 1, 0, 0:INNER]
        wx_raw = ch[:, 1, 1, :].rearrange("p (g e) -> p g e", g=2)
        wdt_raw = ch[:, 2, 0, :].rearrange("p (g a r) -> p g a r", g=2, a=DT)
        z_last = hs[:, :, :, :].rearrange("p a b t -> p (a b t)").rearrange("p (j m) -> p j m", m=P)
        stats_last = ch[:, 0, 0, 0:TILES * 6].rearrange("p (j s) -> p j s", s=6)
        mv_last = ch[:, 0, 1, 0:TILES * 2].rearrange("p (j s) -> p j s", s=2)
        rstd_last = ch[:, 1, 0, 0:TILES]

        y_ps = pb("y_ps", [P, DT, CHUNK])
        da_ps = pb("da_ps", [P, DT, CHUNK])
        b_ps = pb("b_ps", [P, CHUNK])
        c_ps = pb("c_ps", [P, 2, CHUNK])
        pre = pb("pre", [P, CHUNK])

        (weights_in, cols_in, ident_zero, ident_ready, pads_ready, raw_zero, half_ready, small_dve, select_sum, select_ready, weights_ps,
         weights_sb, a_exp, a_ready, diag_ready, h_in_ready, h_res_ready, ht_ps, ht_sb, x_ps, x_sb, z_ps,
         z_raw, silu_z_ready, tap0, conv, xs_ready, x_dbl_ps, x_dbl_sb, bc_hi, bc_rest_ready, bc_mid, bc_ready,
         u_ps, u_taken, sp_e_ready, sp_l_ready, sp_square, sp_cube, sp_min, dt_ready, dtx_ready,
         b_ps_ready, b_sb_ready, dbx_ready, da_ready, scanned, carried, c_ps_ready, c_sb_ready, ch_vector,
         ch_pool, summed, y_saved, g_ready, o_ps, resid_ready, stats_ready, mv1_ready,
         rstd1_ready, x1_ready, x1_kept, mv2_ready, rstd2_ready, xn_ready, xn_ps, xn_sb, max_ready, all_max,
         w_sum, w_sum_all, wq_ready, scaled, scale_ready, clipped, out_ps, z_ready, mv_last_ready,
         rstd_last_ready, final_ready, stored) = [sem(n) for n in (
             "weights_in cols_in ident_zero ident_ready pads_ready raw_zero half_ready small_dve select_sum select_ready weights_ps "
             "weights_sb a_exp a_ready diag_ready h_in_ready h_res_ready ht_ps ht_sb x_ps x_sb z_ps "
             "z_raw silu_z_ready tap0 conv xs_ready x_dbl_ps x_dbl_sb bc_hi bc_rest_ready bc_mid bc_ready "
             "u_ps u_taken sp_e_ready sp_l_ready sp_square sp_cube sp_min dt_ready dtx_ready "
             "b_ps_ready b_sb_ready dbx_ready da_ready scanned carried c_ps_ready c_sb_ready ch_vector "
             "ch_pool summed y_saved g_ready o_ps resid_ready stats_ready mv1_ready "
             "rstd1_ready x1_ready x1_kept mv2_ready rstd2_ready xn_ready xn_ps xn_sb max_ready all_max "
             "w_sum w_sum_all wq_ready scaled scale_ready clipped out_ps z_ready mv_last_ready "
             "rstd_last_ready final_ready stored").split()]

        block = ctx.enter_context(nc.Block())

        def following(b, s):
            return (b, s + 1) if s + 1 < NG else (b + 1, 0)

        def batches(eng, body):
            body(0, True, False)
            with eng.Fori(1, BATCH - 1) as b:
                body(b, False, False)
            body(BATCH - 1, False, True)

        def wait_c_product(eng, b, s, n):
            group = NG * b + s
            if n in POOL_C:
                eng.wait_ge(ch_pool, NPC * group + pool_c_before(n) + 1)
            else:
                eng.wait_ge(ch_vector, NVC * group + vector_c_before(n) + 1)

        def chunk_of(s):
            c = GROUPS[s][1]
            return slice(c * CHUNK, (c + 1) * CHUNK)

        def in_scan_order(ap, s):
            return ap if GROUPS[s][0] == FWD else ap[:, ::-1]

        def last_column(s):
            return CHUNK - 1 if GROUPS[s][0] == FWD else 0

        @block.sync
        def _(sp):
            sp.dma_start(h_in[:], h_tiles[0]).then_inc(h_in_ready, 16)
            sp.dma_start(w_in_raw, w_in.rearrange("(q p) m -> p q m", p=P)).then_inc(weights_in, 16)
            for g, wx in enumerate((wx_f, wx_r)):
                sp.dma_start(wx_raw[0:32, g, :], wx[RANK:RANK + 32, :]).then_inc(weights_in, 16)
                sp.dma_start(wx_raw[32:64, g, :], wx[RANK:RANK + 32, :]).then_inc(weights_in, 16)
                sp.dma_start(wx_raw[64:128, g, :], wx[0:RANK, :]).then_inc(weights_in, 16)
            for g, wdt in enumerate((wdt_f, wdt_r)):
                sp.dma_start(wdt_raw[:, g, :, RANK:], wdt.rearrange("(a p) r -> p a r", p=P)).then_inc(weights_in, 16)
            sp.dma_start(w_out_raw, w_out).then_inc(weights_in, 16)
            for g, (cw, cb, bd, al, d) in enumerate(((conv_w_f, conv_b_f, bdt_f, alog_f, d_f),
                                                     (conv_w_r, conv_b_r, bdt_r, alog_r, d_r))):
                sp.dma_start(conv_w[:, g], cw.rearrange("(a p) k -> p a k", p=P)).then_inc(cols_in, 16)
                sp.dma_start(conv_b[:, g], cb.rearrange("(a p) -> p a", p=P), allow_slow_non_contiguous=True).then_inc(cols_in, 16)
                sp.dma_start(bdt[:, g], bd.rearrange("(a p) -> p a", p=P), allow_slow_non_contiguous=True).then_inc(cols_in, 16)
                sp.dma_start(neg_a[:, g], al.rearrange("(a p) n -> p a n", p=P)).then_inc(cols_in, 16)
                sp.dma_start(d_col[:, g], d.rearrange("(a p) -> p a", p=P), allow_slow_non_contiguous=True).then_inc(cols_in, 16)
            sp.dma_start(gamma_col[:], ln_gamma.rearrange("(p o) -> p o", o=1)).then_inc(cols_in, 16)
            sp.dma_start(beta_col[:], ln_beta.rearrange("(p o) -> p o", o=1)).then_inc(cols_in, 16)
            sp.dma_start(w_raw[:], w_ffn).then_inc(cols_in, 16)

            def batch(b, first, last):
                if not first:
                    sp.wait_ge(resid_ready, 2 * b)
                sp.dma_start(h_res[:], h_tiles[bass.ds(b, 1)].rearrange("o p t m -> p (o t) m")
                             if not isinstance(b, int) else h_tiles[b]).then_inc(h_res_ready, 16)
                if not last:
                    sp.wait_ge(ht_ps, 2 * b + 2)
                    sp.dma_start(h_in[:], h_tiles[bass.ds(b + 1, 1)].rearrange("o p t m -> p (o t) m")
                                 if not isinstance(b, int) else h_tiles[b + 1]).then_inc(h_in_ready, 16)

            batches(sp, batch)
            for c in range(BATCH):
                sp.wait_ge(final_ready, c + 1)
                tiles = slice(c * TILES // BATCH, (c + 1) * TILES // BATCH)
                sp.dma_start(out_tiles[:, tiles, :], z_last[:, tiles, :]).then_inc(stored, 16)
            sp.wait_ge(stored, 16 * BATCH)

        @block.gpsimd
        def _(pool):
            nc.gpsimd.memset(ident[:], 0.0).then_inc(ident_zero, 1)
            pool.wait_ge(ident_zero, 1)
            nc.gpsimd.affine_select(out=ident[:], in_=ident[:], compare_op=ALU.not_equal, fill=1.0, base=0,
                                    pattern=[[-1, P]], channel_multiplier=1).then_inc(ident_ready, 1)
            nc.gpsimd.memset(wdt_raw[:, :, :, 0:RANK], 0.0).then_inc(raw_zero, 1)
            nc.gpsimd.memset(x_pad[:, :, 0:PAD], 0.0).then_inc(pads_ready, 1)
            nc.gpsimd.memset(x_pad[:, :, PAD + SEQ:], 0.0).then_inc(pads_ready, 1)
            nc.gpsimd.memset(bc_parts[:], 0.0).then_inc(pads_ready, 1)
            nc.gpsimd.memset(above_one[:], 1.0 + 2.0 ** -23).then_inc(pads_ready, 1)
            nc.gpsimd.memset(minus_three_quarters[:], -0.75).then_inc(pads_ready, 1)
            nc.gpsimd.memset(half[:], -0.5).then_inc(half_ready, 1)
            pool.wait_ge(w_sum, 1)
            nc.gpsimd.partition_all_reduce(tiny[:, 1:2], tiny[:, 0:1], P, REDUCE.add).then_inc(w_sum_all, 1)

            def times_b(b, s, n):
                group = NG * b + s
                if n == 0:
                    pool.wait_ge(dtx_ready, group + 1)
                pool.wait_ge(b_sb_ready, STATES * group + n + 1)
                if not (isinstance(group, int) and group == 0 and n < RING):
                    pool.wait_ge(scanned, DT * (STATES * group + n - RING + 1))
                nc.gpsimd.tensor_tensor(dbx[:, n % RING], dtx[:, s % 2],
                                        b_ring[:, n % RING, :].unsqueeze(1).to_broadcast([P, DT, CHUNK]),
                                        ALU.mult).then_inc(dbx_ready, 1)

            def times_c(b, s, n):
                group = NG * b + s
                pool.wait_ge(scanned, DT * (STATES * group + n + 1))
                pool.wait_ge(c_sb_ready, NPC * group + pool_c_before(n) + 1)
                if not (isinstance(group, int) and group == 0 and n < RING):
                    pool.wait_ge(summed, STATES * group + n - RING + 1)
                nc.gpsimd.tensor_tensor(ch[:, n % RING], hs[:, n % RING],
                                        c_ring[:, pool_c_before(n), :].unsqueeze(1).to_broadcast([P, DT, CHUNK]),
                                        ALU.mult).then_inc(ch_pool, 1)

            def inverse_deviation(e, mv, mv_ready, rstd, rstd_ready, eps):
                pool.wait_ge(mv_ready, 2 * (e + 1))
                nc.gpsimd.tensor_tensor(rstd[:], mv[:, :, 1], half[:, 0:TT], ALU.pow).then_inc(rstd_ready, 1)

            def batch(b, first, last):
                for s in range(NG):
                    for n in range(STATES):
                        if n - 1 in POOL_C:
                            times_c(b, s, n - 1)
                        if n + 2 < STATES:
                            times_b(b, s, n + 2)
                        elif not (last and s == NG - 1):
                            times_b(*following(b, s), n + 2 - STATES)
                        if s == NG - 1 or (s == 0 and not first):
                            e = 2 * b if s else 2 * b - 1
                            if n == 7:
                                inverse_deviation(e, mv1, mv1_ready, rstd1, rstd1_ready, LN1_EPS)
                            if n == 10:
                                inverse_deviation(e, mv2, mv2_ready, rstd2, rstd2_ready, LN2_EPS)

            times_b(0, 0, 0)
            times_b(0, 0, 1)
            batches(pool, batch)
            e = 2 * BATCH - 1
            inverse_deviation(e, mv1, mv1_ready, rstd1, rstd1_ready, LN1_EPS)
            inverse_deviation(e, mv2, mv2_ready, rstd2, rstd2_ready, LN2_EPS)
            pool.wait_ge(max_ready, 2 * BATCH + 1)
            nc.gpsimd.partition_all_reduce(tiny[:, 5:6], tiny[:, 4:5], P, REDUCE.max).then_inc(all_max, 1)
            for c in range(BATCH):
                pool.wait_ge(mv_last_ready, 2 * (c + 1))
                t = slice(c * TILES // BATCH, (c + 1) * TILES // BATCH)
                nc.gpsimd.tensor_tensor(rstd_last[:, t], mv_last[:, t, 1], half[:, t],
                                        ALU.pow).then_inc(rstd_last_ready, 1)

        @block.scalar
        def _(act):
            nc.scalar.preload_act_table_set(EXP_LN)
            act.wait_ge(cols_in, 16 * 13)
            nc.scalar.activation(neg_a[:], neg_a[:], ACT.Exp).then_inc(a_exp, 1)
            act.wait_ge(weights_ps, 4)
            nc.scalar.copy(w_in_t[:], y_ps[:, 0, :]).then_inc(weights_sb, 1)
            nc.scalar.copy(w_mix_t[:].rearrange("p a m -> p (a m)"), y_ps[:, 1, :]).then_inc(weights_sb, 1)
            nc.scalar.copy(wx_rev_t[:].rearrange("p a m -> p (a m)"), da_ps[:, 0, 0:2 * P]).then_inc(weights_sb, 1)
            nc.scalar.copy(wdt_t[:].rearrange("p g a m -> p (g a m)"), da_ps[:, 1, :]).then_inc(weights_sb, 1)

            def copy_ht(b, c):
                act.wait_ge(ht_ps, CHUNKS * b + c + 1)
                nc.scalar.copy(h_t[:, c * CHUNK:(c + 1) * CHUNK], pre[:]).then_inc(ht_sb, 1)

            def copy_x(b, j):
                a, c = divmod(j, CHUNKS)
                if j == 0 and not (isinstance(b, int) and b == 0):
                    act.wait_ge(conv, 6 * NG * b)
                act.wait_ge(x_ps, DT * CHUNKS * b + j + 1)
                nc.scalar.copy(x_pad[:, a, PAD + c * CHUNK:PAD + (c + 1) * CHUNK], pre[:]).then_inc(x_sb, 1)

            def copy_z(b, j):
                a, c = divmod(j, CHUNKS)
                if j == 0 and not (isinstance(b, int) and b == 0):
                    act.wait_ge(g_ready, CHUNKS * b)
                act.wait_ge(z_ps, DT * CHUNKS * b + j + 1)
                nc.scalar.copy(silu_z[:, a, c * CHUNK:(c + 1) * CHUNK], pre[:]).then_inc(z_raw, 1)

            def prepare(b, s, n, silu_gate=None):
                q = NG * b + s
                g, c = GROUPS[s]
                par = s % 2
                zero = isinstance(q, int) and q == 0
                if n == 0:
                    act.wait_ge(x_sb, DT * CHUNKS * (b + 1))
                    if zero:
                        act.wait_ge(pads_ready, 5)
                    if not (isinstance(q, int) and q < 2):
                        act.wait_ge(summed, STATES * (q - 1))
                        act.wait_ge(dtx_ready, q - 1)
                    for a in range(DT):
                        at = c * CHUNK + (0 if g == FWD else 2 * PAD)
                        nc.scalar.activation(xs[:, par, a, :], x_pad[:, a, at:at + CHUNK], ACT.Identity,
                                             scale=conv_w[:, g, a, 0:1], bias=conv_b[:, g, a:a + 1]).then_inc(tap0, 1)
                if n == 2:
                    act.wait_ge(conv, 6 * (q + 1))
                    nc.scalar.activation(xs[:, par], xs[:, par], ACT.Silu).then_inc(xs_ready, 1)
                    if silu_gate is not None:
                        act.wait_ge(z_raw, DT * CHUNKS * (silu_gate + 1))
                        nc.scalar.activation(silu_z[:], silu_z[:], ACT.Silu).then_inc(silu_z_ready, 1)
                    nc.scalar.preload_act_table_set(EXP_LN)
                if n == 4:
                    act.wait_ge(x_dbl_ps, q + 1)
                    if not zero:
                        act.wait_ge(u_ps, 2 * q)
                        act.wait_ge(bc_rest_ready, q)
                    nc.scalar.copy(x_dbl[:], pre[:]).then_inc(x_dbl_sb, 1)
                    if not (isinstance(q, int) and q < 2):
                        act.wait_ge(c_ps_ready, STATES * (q - 1))
                    nc.scalar.copy(bc_parts[0:64, par], pre[0:64, :]).then_inc(bc_hi, 1)
                if n == 5:
                    act.wait_ge(bc_rest_ready, q + 1)
                    nc.scalar.copy(bc_parts[32:64, par], bc_rest[32:64, :]).then_inc(bc_mid, 1)
                if n in (7, 9):
                    a = (n - 7) // 2
                    act.wait_ge(u_ps, 2 * q + a + 1)
                    if not zero and a == 0:
                        act.wait_ge(dt_ready, q)
                    nc.scalar.activation(sp_e[:, a], pre[:], ACT.Abs, bias=bdt[:, g, a:a + 1]).then_inc(u_taken, 1)
                    nc.scalar.activation(sp_r[:, a], pre[:], ACT.Relu, bias=bdt[:, g, a:a + 1]).then_inc(u_taken, 1)
                if n == 9:
                    act.wait_ge(u_taken, 4 * (q + 1))
                    nc.scalar.activation(sp_e[:], sp_e[:], ACT.Exp, scale=-1.0).then_inc(sp_e_ready, 1)
                if n == 10:
                    act.wait_ge(sp_e_ready, q + 1)
                    nc.scalar.activation(sp_s[:], sp_e[:], ACT.Square, bias=minus_three_quarters[:]).then_inc(sp_square, 1)
                    nc.scalar.activation(sp_l[:], sp_e[:], ACT.Ln, bias=above_one[:]).then_inc(sp_l_ready, 1)

            def copy_b(b, s, n):
                group = NG * b + s
                act.wait_ge(b_ps_ready, STATES * group + n + 1)
                if not (isinstance(group, int) and group == 0 and n < RING):
                    act.wait_ge(dbx_ready, STATES * group + n - RING + 1)
                nc.scalar.copy(b_ring[:, n % RING, :], b_ps[:]).then_inc(b_sb_ready, 1)

            def keep_x1(b_e, h_e):
                e = 2 * b_e + h_e
                act.wait_ge(x1_ready, TT * (e + 1))
                tile = (SEQ // P) * b_e + (1 - h_e) * TT
                dst = x1[:, tile:tile + TT, :] if isinstance(tile, int) else x1[:, bass.ds(tile, TT), :]
                nc.scalar.copy(dst, xn[:]).then_inc(x1_kept, 1)

            def norm_out(b_e, h_e):
                e = 2 * b_e + h_e
                act.wait_ge(xn_ps, e + 1)
                col = (SEQ * b_e + (1 - h_e) * CHUNK)
                dst = xn_t[:, col:col + CHUNK] if isinstance(col, int) else xn_t[:, bass.ds(col, CHUNK)]
                nc.scalar.activation(dst, pre[:], ACT.Identity,
                                     scale=gamma_col[:], bias=beta_col[:]).then_inc(xn_sb, 1)

            def batch(b, first, last):
                for s in range(NG):
                    group = NG * b + s
                    g, c = GROUPS[s]
                    if not first and s == 0:
                        nc.scalar.preload_act_table_set(EXP_LN)
                    for n in range(STATES):
                        for a in range(DT):
                            if n == 0 and a == 0:
                                act.wait_ge(dt_ready, group + 1)
                            if not (isinstance(group, int) and group == 0 and n == 0):
                                act.wait_ge(scanned, DT * (STATES * group + n - 1) + a + 1)
                            nc.scalar.activation(da_ps[:, a, :], dt[:, s % 2, a, :], ACT.Exp,
                                                 scale=neg_a[:, g, a, n:n + 1]).then_inc(da_ready, 1)
                        if n == 2 and s == 1:
                            act.wait_ge(summed, STATES * group)
                            nc.scalar.copy(y_fwd[:], y_ps[:]).then_inc(y_saved, 1)
                        if n + LEAD < STATES:
                            copy_b(b, s, n + LEAD)
                        elif not (last and s == NG - 1):
                            copy_b(*following(b, s), n + LEAD - STATES)
                        if n in POOL_C:
                            act.wait_ge(c_ps_ready, STATES * group + n + 1)
                            if not (isinstance(group, int) and group == 0):
                                act.wait_ge(ch_pool, NPC * (group - 1) + pool_c_before(n) + 1)
                            nc.scalar.copy(c_ring[:, pool_c_before(n), :], c_ps[:, n % 2, :]).then_inc(c_sb_ready, 1)
                        if not (last and s == NG - 1):
                            prepare(*following(b, s), n, silu_gate=b if s == 2 else None)
                        if s == 1 and n in (10, 11, 12, 13):
                            copy_z(b, n - 10)
                        if s == 2 and not last:
                            if n in (10, 11):
                                copy_ht(b + 1, n - 10)
                            if n in (12, 13, 14, 15):
                                copy_x(b + 1, n - 12)
                        if s == NG - 1 or (s == 0 and not first):
                            of, h_e = (b, 0) if s else (b - 1, 1)
                            if n == 9:
                                keep_x1(of, h_e)
                            if n == 14:
                                norm_out(of, h_e)

            copy_ht(0, 0)
            copy_ht(0, 1)
            for j in range(DT * CHUNKS):
                copy_x(0, j)
            for n in range(STATES):
                prepare(0, 0, n)
            for n in range(LEAD):
                copy_b(0, 0, n)
            batches(act, batch)
            keep_x1(BATCH - 1, 1)
            norm_out(BATCH - 1, 1)
            act.wait_ge(scale_ready, 1)
            for c in range(2 * BATCH):
                t = slice(c * CHUNK, (c + 1) * CHUNK)
                nc.scalar.activation(xn_t[:, t], xn_t[:, t], ACT.Copy, scale=tiny[:, 7:8]).then_inc(scaled, 1)

        @block.vector
        def _(dve):
            small = [0]

            def chained(ins):
                small[0] += 1
                ins.then_inc(small_dve, 1)
                dve.wait_ge(small_dve, small[0])

            dve.wait_ge(ident_ready, 1)
            chained(nc.vector.tensor_tensor(xn[:, 0, 0:32], ident[:, 0:32], ident[:, 32:64], ALU.add))
            chained(nc.vector.tensor_tensor(xn[:, 0, 0:32], xn[:, 0, 0:32], ident[:, 64:96], ALU.add))
            nc.vector.tensor_copy(select[:], xn[:, 0, 0:32].unsqueeze(2).to_broadcast([P, 2 * STATES, P])
                                  ).then_inc(select_ready, 1)
            dve.wait_ge(a_exp, 1)
            nc.vector.tensor_scalar(neg_a[:], neg_a[:], -1.0, None, ALU.mult).then_inc(a_ready, 1)
            for g in range(2):
                for a in range(DT):
                    nc.vector.tensor_scalar(diag_d[:, g, a, :], ident[:], d_col[:, g, a:a + 1], None,
                                            ALU.mult).then_inc(diag_ready, 1)
            nc.vector.tensor_reduce(tiny[:, 0:1], w_raw[:], X, ALU.add, apply_absolute_value=True).then_inc(w_sum, 1)

            def quantise_weight():
                dve.wait_ge(w_sum_all, 1)
                chained(nc.vector.tensor_scalar(tiny[:, 2:3], tiny[:, 1:2], 1.0 / (P * P), None, ALU.mult))
                chained(nc.vector.tensor_scalar(tiny[:, 3:4], tiny[:, 2:3], QUANT_EPS, None, ALU.add))
                chained(nc.vector.reciprocal(tiny[:, 3:4], tiny[:, 3:4]))
                chained(nc.vector.tensor_scalar(w_q[:], w_raw[:], tiny[:, 3:4], ROUND, ALU.mult, ALU.add))
                chained(nc.vector.tensor_scalar(w_q[:], w_q[:], ROUND, 1.0, ALU.subtract, ALU.min))
                nc.vector.tensor_scalar(w_q[:], w_q[:], -1.0, None, ALU.max).then_inc(wq_ready, 1)

            def prepare(b, s, n):
                q = NG * b + s
                g, c = GROUPS[s]
                par = s % 2
                for k in ((1,), (2, 3))[n] if n < 2 else ():
                    for a in range(DT):
                        if k == 1:
                            dve.wait_ge(tap0, DT * q + a + 1)
                        else:
                            dve.wait_ge(conv, 6 * q + DT * (k - 2) + a + 1)
                        at = c * CHUNK + (k if g == FWD else 2 * PAD - k)
                        nc.vector.scalar_tensor_tensor(xs[:, par, a, :], x_pad[:, a, at:at + CHUNK],
                                                       conv_w[:, g, a, k:k + 1], xs[:, par, a, :],
                                                       ALU.mult, ALU.add).then_inc(conv, 1)
                if n == 4:
                    dve.wait_ge(x_dbl_sb, q + 1)
                    dve.wait_ge(bc_hi, q + 1)
                    nc.vector.tensor_tensor(bc_rest[:], x_dbl[0:64, :], bc_parts[0:64, par],
                                            ALU.subtract).then_inc(bc_rest_ready, 1)
                if n == 5:
                    dve.wait_ge(bc_mid, q + 1)
                    nc.vector.tensor_tensor(bc_parts[64:96, par], bc_rest[32:64, :], bc_parts[32:64, par],
                                            ALU.subtract).then_inc(bc_ready, 1)
                if n == 11:
                    dve.wait_ge(sp_square, q + 1)
                    nc.vector.scalar_tensor_tensor(sp_s[:], sp_s[:], 39.0 / 16.0, sp_e[:],
                                                   ALU.add, ALU.mult).then_inc(sp_cube, 1)
                if n == 12:
                    dve.wait_ge(sp_cube, q + 1)
                    dve.wait_ge(sp_l_ready, q + 1)
                    nc.vector.scalar_tensor_tensor(sp_s[:], sp_l[:], 3.0, sp_s[:],
                                                   ALU.mult, ALU.min).then_inc(sp_min, 1)
                    dve.wait_ge(sp_min, q + 1)
                    if not (isinstance(q, int) and q < 2):
                        dve.wait_ge(da_ready, DT * STATES * (q - 1))
                    nc.vector.scalar_tensor_tensor(dt[:, par], sp_s[:], 1.0 / 3.0, sp_r[:],
                                                   ALU.mult, ALU.add).then_inc(dt_ready, 1)
                if n == 13:
                    dve.wait_ge(dt_ready, q + 1)
                    dve.wait_ge(xs_ready, q + 1)
                    if not (isinstance(q, int) and q < 2):
                        dve.wait_ge(dbx_ready, STATES * (q - 1))
                    nc.vector.tensor_tensor(dtx[:, par], dt[:, par], xs[:, par], ALU.mult).then_inc(dtx_ready, 1)

            def times_c(b, s, n):
                group = NG * b + s
                dve.wait_ge(c_ps_ready, STATES * group + n + 1)
                dve.wait_ge(scanned, DT * (STATES * group + n + 1))
                if not (isinstance(group, int) and group == 0 and n < RING):
                    dve.wait_ge(summed, STATES * group + n - RING + 1)
                nc.vector.tensor_tensor(ch[:, n % RING], hs[:, n % RING],
                                        c_ps[:, n % 2, :].unsqueeze(1).to_broadcast([P, DT, CHUNK]),
                                        ALU.mult).then_inc(ch_vector, 1)

            def keep_state(b, s, n):
                dve.wait_ge(scanned, DT * (STATES * (NG * b + s) + n + 1))
                nc.vector.tensor_copy(carry[:, :, n:n + 1],
                                      hs[:, n % RING, :, last_column(s):last_column(s) + 1]).then_inc(carried, 1)

            def gate(b, s):
                e = 2 * b + (1 if s == 3 else 0)
                dve.wait_ge(summed, STATES * (NG * b + s + 1))
                dve.wait_ge(silu_z_ready, b + 1)
                if not (isinstance(e, int) and e == 0):
                    dve.wait_ge(o_ps, e)
                nc.vector.tensor_tensor(gated[:], y_ps[:], silu_z[:, :, chunk_of(s)], ALU.mult).then_inc(g_ready, 1)

            def statistics(source, e, layer):
                for j in range(TT):
                    nc.vector.bn_stats(stats[:, j, :], source[:, j, :]).then_inc(stats_ready, 1)

            def statistics_wait(e, layer):
                dve.wait_ge(stats_ready, 2 * TT * e + TT * (layer + 1))

            def aggregate(e, layer):
                mv, mv_ready, eps = ((mv1, mv1_ready, LN1_EPS), (mv2, mv2_ready, LN2_EPS))[layer]
                for j in range(TT):
                    ins = nc.vector.bn_aggr(mv[:, j, :], stats[:, j, :])
                ins.then_inc(mv_ready, 1)
                dve.wait_ge(mv_ready, 2 * e + 1)
                nc.vector.tensor_scalar(mv[:, :, 1], mv[:, :, 1], eps, None, ALU.add).then_inc(mv_ready, 1)

            def norm_step(b, h_e, n):
                e = 2 * b + h_e
                tile0 = (1 - h_e) * TT
                if n == 5:
                    dve.wait_ge(h_res_ready, 16 * (b + 1))
                    dve.wait_ge(o_ps, e + 1)
                    nc.vector.tensor_tensor(resid[:], pre[:].rearrange("p (t m) -> p t m", t=TT),
                                            h_res[:, tile0:tile0 + TT, :], ALU.add).then_inc(resid_ready, 1)
                    dve.wait_ge(resid_ready, e + 1)
                    statistics(resid, e, 0)
                if n == 6:
                    aggregate(e, 0)
                if n == 8:
                    dve.wait_ge(rstd1_ready, e + 1)
                    for j in range(TT):
                        nc.vector.tensor_scalar(xn[:, j, :], resid[:, j, :], mv1[:, j, 0:1], rstd1[:, j:j + 1],
                                                ALU.subtract, ALU.mult).then_inc(x1_ready, 1)
                    dve.wait_ge(x1_ready, TT * (e + 1))
                    statistics(xn, e, 1)
                if n == 9:
                    aggregate(e, 1)
                if n == 11:
                    dve.wait_ge(x1_kept, e + 1)
                    dve.wait_ge(rstd2_ready, e + 1)
                    for j in range(TT):
                        nc.vector.tensor_scalar(xn[:, j, :], xn[:, j, :], mv2[:, j, 0:1], rstd2[:, j:j + 1],
                                                ALU.subtract, ALU.mult).then_inc(xn_ready, 1)
                if n == 15:
                    dve.wait_ge(xn_sb, e + 1)
                    col = SEQ * b + (1 - h_e) * CHUNK
                    slot = part_max[:, e:e + 1] if isinstance(e, int) else part_max[:, bass.ds(e, 1)]
                    src = xn_t[:, col:col + CHUNK] if isinstance(col, int) else xn_t[:, bass.ds(col, CHUNK)]
                    nc.vector.tensor_reduce(slot, src, X, ALU.max, apply_absolute_value=True).then_inc(max_ready, 1)

            def batch(b, first, last):
                for s in range(NG):
                    group = NG * b + s
                    g, c = GROUPS[s]
                    starts = s in (0, 2)
                    for n in range(STATES):
                        if n in (6, 9):
                            if s == NG - 1:
                                statistics_wait(2 * b, n // 9)
                            if s == 0 and not first:
                                statistics_wait(2 * b - 1, n // 9)
                        for a in range(DT):
                            idx = STATES * group + n
                            dve.wait_ge(da_ready, DT * idx + a + 1)
                            if a == 0:
                                dve.wait_ge(dbx_ready, idx + 1)
                                if n >= RING:
                                    wait_c_product(dve, b, s, n - RING)
                                elif not (first and s == 0):
                                    pb_, ps_ = (b, s - 1) if s else (b - 1, NG - 1)
                                    wait_c_product(dve, pb_, ps_, n - RING + STATES)
                            if starts:
                                initial = 0.0
                            else:
                                initial = carry[:, a, n:n + 1]
                                if n == 0 and a == 0:
                                    dve.wait_ge(carried, STATES * (2 * b + s // 2) + 1)
                                elif a == 0:
                                    dve.wait_ge(carried, STATES * (2 * b + s // 2) + n + 1)
                            nc.vector.tensor_tensor_scan(in_scan_order(hs[:, n % RING, a, :], s),
                                                         in_scan_order(da_ps[:, a, :], s),
                                                         in_scan_order(dbx[:, n % RING, a, :], s),
                                                         initial, ALU.mult, ALU.add).then_inc(scanned, 1)
                        if n:
                            prev = (b, s, n - 1)
                        else:
                            prev = (b, s - 1, STATES - 1) if s else (b - 1, NG - 1, STATES - 1)
                        if n == 2 and s == 3:
                            gate(b, 2)
                        if n == 2 and s == 0 and not first:
                            gate(b - 1, 3)
                        if not (first and s == 0 and n == 0):
                            if prev[1] in (0, 2):
                                keep_state(*prev)
                            if prev[2] not in POOL_C:
                                times_c(*prev)
                        if not (last and s == NG - 1):
                            prepare(*following(b, s), n)
                        if s == NG - 1:
                            norm_step(b, 0, n)
                        if s == 0 and not first:
                            norm_step(b - 1, 1, n)
                        if first and s == 1 and n == 4:
                            quantise_weight()

            for n in range(STATES):
                prepare(0, 0, n)
            batches(dve, batch)
            times_c(BATCH - 1, NG - 1, STATES - 1)
            gate(BATCH - 1, 3)
            for n in range(STATES):
                if n in (6, 9):
                    statistics_wait(2 * BATCH - 1, n // 9)
                norm_step(BATCH - 1, 1, n)
            dve.wait_ge(max_ready, 2 * BATCH)
            nc.vector.tensor_reduce(tiny[:, 4:5], part_max[:], X, ALU.max).then_inc(max_ready, 1)
            dve.wait_ge(all_max, 1)
            chained(nc.vector.reciprocal(tiny[:, 6:7], tiny[:, 5:6]))
            nc.vector.tensor_scalar(tiny[:, 7:8], tiny[:, 6:7], QB, None, ALU.mult).then_inc(scale_ready, 1)
            chained(nc.vector.tensor_scalar(tiny[:, 8:9], tiny[:, 5:6], tiny[:, 2:3], 1.0 / QB, ALU.mult, ALU.mult))

            def last_norm(c):
                per = TILES // BATCH
                t0 = c * per
                for i in range(2):
                    j = 2 * c + i
                    dve.wait_ge(out_ps, j + 1)
                    t = slice(j * TT, (j + 1) * TT)
                    bank = c_ps[:, j % 2, :]
                    nc.vector.scalar_tensor_tensor(z_last[:, t, :].rearrange("p t m -> p (t m)"), bank,
                                                   tiny[:, 8:9], x1[:, t, :].rearrange("p t m -> p (t m)"),
                                                   ALU.mult, ALU.add).then_inc(z_ready, 1)
                    dve.wait_ge(z_ready, j + 1)
                    for m in range(TT):
                        nc.vector.bn_stats(stats_last[:, j * TT + m, :], z_last[:, j * TT + m, :]).then_inc(stats_ready, 1)
                dve.wait_ge(stats_ready, 2 * TT * 2 * BATCH + per * (c + 1))
                for m in range(per):
                    ins = nc.vector.bn_aggr(mv_last[:, t0 + m, :], stats_last[:, t0 + m, :])
                ins.then_inc(mv_last_ready, 1)
                dve.wait_ge(mv_last_ready, 2 * c + 1)
                nc.vector.tensor_scalar(mv_last[:, t0:t0 + per, 1], mv_last[:, t0:t0 + per, 1], LN1_EPS, None,
                                        ALU.add).then_inc(mv_last_ready, 1)
                dve.wait_ge(rstd_last_ready, c + 1)
                for m in range(t0, t0 + per):
                    ins = nc.vector.tensor_scalar(z_last[:, m, :], z_last[:, m, :], mv_last[:, m, 0:1],
                                                  rstd_last[:, m:m + 1], ALU.subtract, ALU.mult)
                ins.then_inc(final_ready, 1)

            def clip(c):
                dve.wait_ge(scaled, c + 1)
                t = slice(c * CHUNK, (c + 1) * CHUNK)
                nc.vector.tensor_scalar(xn_t[:, t], xn_t[:, t], QB - QUANT_EPS, -QB + QUANT_EPS,
                                        ALU.min, ALU.max).then_inc(clipped, 1)

            clip(0)
            clip(1)
            for c in range(BATCH):
                if c + 1 < BATCH:
                    clip(2 * c + 2)
                    clip(2 * c + 3)
                last_norm(c)

        @block.tensor
        def _(pe):
            pe.wait_ge(ident_ready, 1)
            pe.wait_ge(raw_zero, 1)
            pe.wait_ge(weights_in, 16 * 10)
            for q in range(4):
                ins = nc.tensor.transpose(y_ps[:, 0, q * P:(q + 1) * P], w_in_raw[:, q, :], ident[:])
            ins.then_inc(weights_ps, 1)
            for a in range(DT):
                nc.tensor.transpose(y_ps[:, 1, a * P:(a + 1) * P], w_out_raw[:, a * P:(a + 1) * P], ident[:])
                ins = nc.tensor.transpose(y_ps[:, 1, (2 + a) * P:(3 + a) * P], wx_raw[:, 0, a * P:(a + 1) * P], ident[:])
            ins.then_inc(weights_ps, 1)
            for a in range(DT):
                ins = nc.tensor.transpose(da_ps[:, 0, a * P:(a + 1) * P], wx_raw[:, 1, a * P:(a + 1) * P], ident[:])
            ins.then_inc(weights_ps, 1)
            for g in range(2):
                for a in range(DT):
                    k = DT * g + a
                    ins = nc.tensor.transpose(da_ps[:, 1, k * P:(k + 1) * P], wdt_raw[:, g, a, :], ident[:])
            ins.then_inc(weights_ps, 1)

            def wx_half(g, a):
                return w_mix_t[:, 2 + a, :] if g == FWD else wx_rev_t[:, a, :]

            def transpose_h(b, c):
                if c == 0:
                    pe.wait_ge(h_in_ready, 16 * (b + 1))
                    if not (isinstance(b, int) and b == 0):
                        pe.wait_ge(z_raw, DT * CHUNKS * b)
                        pe.wait_ge(u_taken, 4 * NG * b)
                else:
                    pe.wait_ge(ht_sb, CHUNKS * b + c)
                for t in range(TT):
                    ins = nc.tensor.transpose(pre[:, t * P:(t + 1) * P], h_in[:, c * TT + t, :], ident[:])
                ins.then_inc(ht_ps, 1)

            def project_x(b, j):
                a, c = divmod(j, CHUNKS)
                if j == 0:
                    pe.wait_ge(ht_sb, CHUNKS * (b + 1))
                else:
                    pe.wait_ge(x_sb, DT * CHUNKS * b + j)
                nc.tensor.matmul(pre[:], w_in_t[:, a * P:(a + 1) * P], h_t[:, c * CHUNK:(c + 1) * CHUNK],
                                 start=True, stop=True).then_inc(x_ps, 1)

            def project_z(b, j):
                a, c = divmod(j, CHUNKS)
                if j == 0:
                    pe.wait_ge(u_taken, 4 * (NG * b + 3))
                else:
                    pe.wait_ge(z_raw, DT * CHUNKS * b + j)
                nc.tensor.matmul(pre[:], w_in_t[:, INNER + a * P:INNER + (a + 1) * P],
                                 h_t[:, c * CHUNK:(c + 1) * CHUNK], start=True, stop=True).then_inc(z_ps, 1)

            def prepare(b, s, n, pre_before, norm_e=None):
                q = NG * b + s
                g, c = GROUPS[s]
                par = s % 2
                if n == 3:
                    pe.wait_ge(xs_ready, q + 1)
                    pe.wait_ge(*pre_before)
                    for a in range(DT):
                        ins = nc.tensor.matmul(pre[:], wx_half(g, a), xs[:, par, a, :], start=a == 0, stop=a == DT - 1)
                    ins.then_inc(x_dbl_ps, 1)
                if n in (6, 8):
                    a = (n - 6) // 2
                    if a == 0:
                        pe.wait_ge(x_dbl_sb, q + 1)
                        if norm_e is None:
                            pe.wait_ge(bc_hi, q + 1)
                        else:
                            pe.wait_ge(resid_ready, norm_e + 1)
                    else:
                        pe.wait_ge(u_taken, 4 * q + 2)
                    nc.tensor.matmul(pre[:], wdt_t[:, g, a, :], x_dbl[:], start=True, stop=True).then_inc(u_ps, 1)

            def broadcast_b(b, s, n):
                group = NG * b + s
                if n == 0:
                    pe.wait_ge(bc_ready, group + 1)
                if not (isinstance(group, int) and group == 0 and n == 0):
                    pe.wait_ge(b_sb_ready, STATES * group + n)
                nc.tensor.matmul(b_ps[:], select[:, n, :], bc_parts[:, s % 2], start=True, stop=True).then_inc(b_ps_ready, 1)

            def broadcast_c(b, s, n, first):
                group = NG * b + s
                if n >= 2 and (n - 2) in POOL_C:
                    pe.wait_ge(c_sb_ready, NPC * group + pool_c_before(n - 1))
                elif n >= 2:
                    pe.wait_ge(ch_vector, NVC * group + vector_c_before(n - 1))
                elif not (first and s == 0):
                    m = n - 2 + STATES
                    if m in POOL_C:
                        pe.wait_ge(c_sb_ready, NPC * (group - 1) + pool_c_before(m + 1))
                    else:
                        pe.wait_ge(ch_vector, NVC * (group - 1) + vector_c_before(m + 1))
                nc.tensor.matmul(c_ps[:, n % 2, :], select[:, STATES + n, :], bc_parts[:, s % 2],
                                 start=True, stop=True).then_inc(c_ps_ready, 1)

            def add_state(b, s, n):
                wait_c_product(pe, b, s, n)
                for a in range(DT):
                    ins = nc.tensor.matmul(y_ps[:, a, :], ident[:], ch[:, n % RING, a, :], start=False,
                                           stop=n == STATES - 1 and s != 1)
                ins.then_inc(summed, 1)

            def start_sum(b, s, first):
                g, c = GROUPS[s]
                if s == 0 and first:
                    pe.wait_ge(weights_sb, 2)
                    pe.wait_ge(diag_ready, 4)
                elif s == 0:
                    pe.wait_ge(g_ready, CHUNKS * b)
                elif s == 1:
                    pe.wait_ge(y_saved, b + 1)
                elif s == 3:
                    pe.wait_ge(g_ready, CHUNKS * b + 1)
                for a in range(DT):
                    nc.tensor.matmul(y_ps[:, a, :], diag_d[:, g, a, :], xs[:, s % 2, a, :], start=s != 2, stop=False)
                    if s == 3:
                        nc.tensor.matmul(y_ps[:, a, :], ident[:], y_fwd[:, a, :], start=False, stop=False)

            def output_product(b, h_e, last):
                e = 2 * b + h_e
                pe.wait_ge(g_ready, e + 1)
                if h_e == 0 and last:
                    pe.wait_ge(u_taken, 4 * NG * BATCH)
                elif h_e == 0:
                    pe.wait_ge(bc_hi, NG * (b + 1) + 1)
                elif last:
                    pe.wait_ge(xn_sb, e)
                else:
                    pe.wait_ge(bc_hi, NG * (b + 1) + 2)
                for t in range(TT):
                    for a in range(DT):
                        ins = nc.tensor.matmul(pre[:, t * P:(t + 1) * P], gated[:, a, t * P:(t + 1) * P],
                                               w_mix_t[:, a, :], start=a == 0, stop=a == DT - 1)
                ins.then_inc(o_ps, 1)

            def transpose_norm(b, h_e, last):
                e = 2 * b + h_e
                pe.wait_ge(xn_ready, TT * (e + 1))
                if last:
                    pe.wait_ge(resid_ready, e + 1)
                elif h_e == 0:
                    pe.wait_ge(u_taken, 4 * (NG * (b + 1) + 1))
                else:
                    pe.wait_ge(u_taken, 4 * (NG * (b + 1) + 2))
                for t in range(TT):
                    ins = nc.tensor.transpose(pre[:, t * P:(t + 1) * P], xn[:, t, :], ident[:])
                ins.then_inc(xn_ps, 1)

            def batch(b, first, last):
                before = ((u_taken, 4 * (NG * b + 1)), (xn_sb, 2 * b) if not first else (u_taken, 8),
                          (z_raw, DT * CHUNKS * (b + 1)), (x_sb, DT * CHUNKS * (b + 2)))
                for s in range(NG):
                    for n in range(STATES):
                        if n + LEAD < STATES:
                            broadcast_b(b, s, n + LEAD)
                        elif not (last and s == NG - 1):
                            broadcast_b(*following(b, s), n + LEAD - STATES)
                        broadcast_c(b, s, n, first)
                        if n == 2:
                            start_sum(b, s, first)
                        if n >= 2:
                            add_state(b, s, n - 2)
                        elif s:
                            add_state(b, s - 1, n - 2 + STATES)
                        elif not first:
                            add_state(b - 1, NG - 1, n - 2 + STATES)
                        norm_e = 2 * b if s == NG - 1 else 2 * b - 1 if s == 0 and not first else None
                        if not (last and s == NG - 1):
                            prepare(*following(b, s), n, before[s], norm_e)
                        if n == 4 and norm_e is not None:
                            output_product(*((b, 0) if s else (b - 1, 1)), last and s == NG - 1)
                        if n == 13 and norm_e is not None:
                            transpose_norm(*((b, 0) if s else (b - 1, 1)), last and s == NG - 1)
                        if s == 1 and n in (9, 10, 11, 12):
                            project_z(b, n - 9)
                        if s == 2 and not last:
                            if n in (9, 10):
                                transpose_h(b + 1, n - 9)
                            if n in (11, 12, 13, 14):
                                project_x(b + 1, n - 11)

            transpose_h(0, 0)
            transpose_h(0, 1)
            pe.wait_ge(weights_sb, 4)
            for j in range(DT * CHUNKS):
                project_x(0, j)
            for n in range(STATES):
                prepare(0, 0, n, (x_sb, DT * CHUNKS))
            pe.wait_ge(select_ready, 1)
            for n in range(LEAD):
                broadcast_b(0, 0, n)
            batches(pe, batch)
            add_state(BATCH - 1, NG - 1, STATES - 2)
            add_state(BATCH - 1, NG - 1, STATES - 1)
            output_product(BATCH - 1, 1, True)
            transpose_norm(BATCH - 1, 1, True)
            pe.wait_ge(wq_ready, 1)
            for j in range(2 * BATCH):
                pe.wait_ge(clipped, j + 1)
                if j >= 2:
                    pe.wait_ge(z_ready, j - 1)
                else:
                    pe.wait_ge(xn_sb, 2 * BATCH)
                bank = c_ps[:, j % 2, :]
                for t in range(TT):
                    k = (j * TT + t) * P
                    ins = nc.tensor.matmul(bank[:, t * P:(t + 1) * P], xn_t[:, k:k + P], w_q[:], start=True, stop=True)
                ins.then_inc(out_ps, 1)


_NAMES = ["L0_attn_hidden_states", "L0_attn_W_in", "L0_attn_W_out", "L0_attn_conv_w_fwd", "L0_attn_conv_b_fwd",
          "L0_attn_Wx_fwd", "L0_attn_Wdt_fwd", "L0_attn_bdt_fwd", "L0_attn_A_log_fwd", "L0_attn_D_fwd",
          "L0_attn_conv_w_rev", "L0_attn_conv_b_rev", "L0_attn_Wx_rev", "L0_attn_Wdt_rev", "L0_attn_bdt_rev",
          "L0_attn_A_log_rev", "L0_attn_D_rev", "L0_ffn_weight", "L0_ffn_ln_gamma", "L0_ffn_ln_beta"]


def kernel(**inputs):
    import numpy as np
    import concourse.bacc as bacc
    from concourse.bass_utils import run_bass_kernel_spmd

    nc = bacc.Bacc("TRN2", target_bir_lowering=False, num_devices=1)
    arrays, args = {}, []
    for name in _NAMES:
        a = np.ascontiguousarray(inputs[name])
        arrays[f"in_{name}"] = a
        args.append(nc.dram_tensor(f"in_{name}", a.shape, mybir.dt.from_np(a.dtype), kind="ExternalInput").ap())
    args.append(nc.dram_tensor("out", (BATCH, SEQ, MODEL), mybir.dt.float32, kind="ExternalOutput").ap())
    build(nc, *args)
    r = run_bass_kernel_spmd(nc, [arrays], core_ids=[0])
    return r.results[0]["out"]
```

```python
import concourse.bass as bass
from concourse import mybir
from contextlib import ExitStack

BATCH, SEQ, MODEL = 4, 1024, 128
INNER, STATES, TAPS, RANK = 256, 16, 4, 64
P = 128
DT = INNER // P
CHUNK = 512
CHUNKS = SEQ // CHUNK
TT = CHUNK // P
TILES = BATCH * SEQ // P
FWD, REV = 0, 1
GROUPS = ((FWD, 0), (FWD, 1), (REV, 1), (REV, 0))
NG = len(GROUPS)
RING = 4
FIRST_STAGES = {"tap0": 10, "tap1": 11, "tap2": 11, "tap3": 13, "silu": 14, "x_dbl": 15}
LATER_STAGES = {"copy x_dbl": 0, "rest": 0, "u0": 1, "u1": 2, "take u0": 2, "middle": 3, "third": 3,
                "take u1": 4, "exp": 5, "square": 7, "series": 6, "ln": 7, "min": 7, "dt": 8, "dtx": 12}
CONVOLVE = (11, 12, 12, 11)
PROJECTIONS = {"z0": 6, "z1": 8, "z2": 4, "z3": 7, "h0": 8, "h1": 10, "x0": 4, "x1": 5, "x2": 8, "x3": 9}
PROJECTIONS_READ = {"z0": 8, "z1": 10, "z2": 6, "z3": 8, "h0": 11, "h1": 12, "x0": 6, "x1": 8, "x2": 10, "x3": 12}
CLOSING = {"save": 3, "start sum": 3, "gate": 1, "output": 4, "residual": 5, "mean1": 6, "deviation1": 6,
           "bias1": 7, "scale1": 8, "statistics2": 8, "mean2": 9, "deviation2": 9, "keep": 9,
           "bias2": 10, "scale2": 11, "transpose": 12, "affine": 14, "largest": 14}
ADDED_AT = ((), (), ()) + ((0,), (1, 2)) + tuple((n - 2,) for n in range(5, STATES))
EXPS_AHEAD = 1
B_AHEAD = 3
DA_BANKS = 3
ROWS_AT = 12
POOL_C = ((1, 6, 11), (2, 6, 11), (0, 6, 10), (1, 6, 11))
NPC = sum(len(states) for states in POOL_C)
NVC = NG * STATES - NPC
C_RING, C_BANKS = 4, 2
LN1_EPS, LN2_EPS, QUANT_EPS, QB = 1e-5, 1e-3, 1e-5, 128.0
ROUND = 1.5 * 2.0 ** 23
EXP_LN, SILU = "natural_log_exp_and_others", "silu_and_others"


def vector_c(b, s, n=0):
    return NVC * b + sum(STATES - len(POOL_C[i]) for i in range(s)) + sum(m not in POOL_C[s] for m in range(n))


def pool_c(b, s, n=0):
    return NPC * b + sum(len(POOL_C[i]) for i in range(s)) + sum(m in POOL_C[s] for m in range(n))


def build(nc, h, w_in, w_out, conv_w_f, conv_b_f, wx_f, wdt_f, bdt_f, alog_f, d_f,
          conv_w_r, conv_b_r, wx_r, wdt_r, bdt_r, alog_r, d_r, w_ffn, ln_gamma, ln_beta, out):
    f32, bf16 = mybir.dt.float32, mybir.dt.bfloat16
    ALU = mybir.AluOpType
    ACT = mybir.ActivationFunctionType
    X = mybir.AxisListType.X
    REDUCE = bass.bass_isa.ReduceOp

    h_tiles = h.rearrange("b (t p) m -> b p t m", p=P)
    out_tiles = out.rearrange("b (t p) m -> p (b t) m", p=P)

    with ExitStack() as ctx:
        def sb(name, shape, dt=f32):
            return ctx.enter_context(nc.sbuf_tensor(name, shape, dt))

        def pb(name, shape):
            return ctx.enter_context(nc.psum_tensor(name, shape, f32))

        def sem(name):
            return ctx.enter_context(nc.semaphore(name))

        ident = sb("ident", [P, P])
        select = sb("select", [P, STATES, P], bf16)
        w_in_t = sb("w_in_t", [P, 2 * INNER])
        w_mix_t = sb("w_mix_t", [P, 4, P])
        wx_rev_t = sb("wx_rev_t", [P, DT, P])
        wdt_t = sb("wdt_t", [P, 2, DT, P])
        diag_d = sb("diag_d", [P, 2, DT, P])
        diag_conv = sb("diag_conv", [P, 2, TAPS, P])
        conv_w = sb("conv_w", [P, 2, DT, TAPS])
        conv_b = sb("conv_b", [P, 2, DT])
        bdt = sb("bdt", [P, 2, DT])
        d_col = sb("d_col", [P, 2, DT])
        neg_a = sb("neg_a", [P, 2, DT, STATES])
        gamma_col = sb("gamma_col", [P, 1])
        beta_col = sb("beta_col", [P, 1])
        w_raw = sb("w_raw", [P, P])
        w_q = sb("w_q", [P, P])
        h_in = sb("h_in", [P, SEQ // P, P])
        h_res = sb("h_res", [P, SEQ // P, P])
        h_t = sb("h_t", [P, SEQ])
        PAD = TAPS - 1
        x_pad = sb("x_pad", [P, DT, PAD + SEQ + PAD])
        silu_z = sb("silu_z", [P, DT, SEQ])
        xs = sb("xs", [P, 2, DT, CHUNK])
        dt = sb("dt", [P, 2, DT, CHUNK])
        dtx = sb("dtx", [P, 2, DT, CHUNK])
        bc_parts = sb("bc_parts", [P, 2, CHUNK], bf16)
        x_dbl = sb("x_dbl", [P, CHUNK])
        bc_rest = sb("bc_rest", [64, CHUNK])
        sp_e = sb("sp_e", [P, DT, CHUNK])
        sp_s = sb("sp_s", [P, DT, CHUNK])
        above_one = sb("above_one", [P, 1])
        minus_three_quarters = sb("minus_three_quarters", [P, 1])
        sp_r = sb("sp_r", [P, DT, CHUNK])
        sp_l = sb("sp_l", [P, DT, CHUNK])
        b_ring = sb("b_ring", [P, RING, CHUNK])
        c_ring = sb("c_ring", [P, C_RING, CHUNK])
        dbx = sb("dbx", [P, RING, DT, CHUNK])
        hs = sb("hs", [P, RING, DT, CHUNK])
        ch = sb("ch", [P, RING, DT, CHUNK])
        carry = sb("carry", [P, DT, STATES])
        y_fwd = sb("y_fwd", [P, DT, CHUNK])
        gated = sb("gated", [P, DT, CHUNK])
        resid = sb("resid", [P, TT, P])
        stats = sb("stats", [P, TT, 6])
        mv1 = sb("mv1", [P, TT, 2])
        mv2 = sb("mv2", [P, TT, 2])
        rstd1 = sb("rstd1", [P, TT])
        rstd2 = sb("rstd2", [P, TT])
        bias1 = sb("bias1", [P, TT])
        bias2 = sb("bias2", [P, TT])
        xn = sb("xn", [P, TT, P])
        x1 = sb("x1", [P, TILES, P])
        xn_t = sb("xn_t", [P, TILES * P])
        part_max = sb("part_max", [P, TILES // TT])
        half = sb("half", [P, TILES])
        tiny = sb("tiny", [P, 16])
        w_in_raw = ch[:, 0, :, :].rearrange("p a t -> p (a t)")[:, 0:4 * P].rearrange("p (q m) -> p q m", q=4)
        w_out_raw = ch[:, 1, 0, 0:INNER]
        wx_raw = ch[:, 1, 1, :].rearrange("p (g e) -> p g e", g=2)
        wdt_raw = ch[:, 2, 0, :].rearrange("p (g a r) -> p g a r", g=2, a=DT)
        z_last = hs[:, :, :, :].rearrange("p a b t -> p (a b t)").rearrange("p (j m) -> p j m", m=P)
        stats_last = ch[:, 0, 0, 0:TILES * 6].rearrange("p (j s) -> p j s", s=6)
        mv_last = ch[:, 0, 1, 0:TILES * 2].rearrange("p (j s) -> p j s", s=2)
        rstd_last = ch[:, 1, 0, 0:TILES]
        bias_last = ch[:, 1, 1, 0:TILES]

        bc_rows = nc.dram_tensor("bc_rows", (NG, 2 * STATES, CHUNK), f32).ap()

        y_ps = pb("y_ps", [P, DT, CHUNK])
        da_ps = pb("da_ps", [P, DA_BANKS, CHUNK])
        c_ps = pb("c_ps", [P, 2, CHUNK])
        pre = pb("pre", [P, CHUNK])

        (w_in_in, conv_in, weights_in, dt_cols_in, cols_in, ident_zero, ident_ready, pads_ready, raw_zero, half_ready, small_dve, select_ready, weights_ps,
         weights_sb, a_exp, a_ready, diag_ready, h_in_ready, h_res_ready, ht_ps, ht_sb, x_ps, x_sb, z_ps,
         z_raw, silu_z_ready, diag_conv_ready, conv_ps, conv_sb, tap0, conv, xs_ready, x_dbl_ps, x_dbl_sb, bc_hi, bc_rest_ready, bc_mid, bc_ready,
         u_ps, u_taken, sp_e_ready, sp_l_ready, sp_square, sp_cube, sp_min, dt_ready, dtx_ready,
         rows_stored, dbx_ready, da_ready, scanned, carried, c_ps_ready, ch_vector,
         ch_pool, summed, y_saved, g_ready, o_ps, resid_ready, stats_ready, mv1_ready,
         rstd1_ready, bias1_ready, x1_ready, x1_kept, mv2_ready, rstd2_ready, bias2_ready, xn_ready, xn_ps, xn_sb, max_ready, all_max,
         w_sum, w_sum_all, wq_ready, bias_last_ready, clipped, out_ps, z_ready, mv_last_ready,
         rstd_last_ready, final_ready, stored) = [sem(n) for n in (
             "w_in_in conv_in weights_in dt_cols_in cols_in ident_zero ident_ready pads_ready raw_zero half_ready small_dve select_ready weights_ps "
             "weights_sb a_exp a_ready diag_ready h_in_ready h_res_ready ht_ps ht_sb x_ps x_sb z_ps "
             "z_raw silu_z_ready diag_conv_ready conv_ps conv_sb tap0 conv xs_ready x_dbl_ps x_dbl_sb bc_hi bc_rest_ready bc_mid bc_ready "
             "u_ps u_taken sp_e_ready sp_l_ready sp_square sp_cube sp_min dt_ready dtx_ready "
             "rows_stored dbx_ready da_ready scanned carried c_ps_ready ch_vector "
             "ch_pool summed y_saved g_ready o_ps resid_ready stats_ready mv1_ready "
             "rstd1_ready bias1_ready x1_ready x1_kept mv2_ready rstd2_ready bias2_ready xn_ready xn_ps xn_sb max_ready all_max "
             "w_sum w_sum_all wq_ready bias_last_ready clipped out_ps z_ready mv_last_ready "
             "rstd_last_ready final_ready stored").split()]

        b_in = [sem(f"b_in{k}") for k in range(RING)]
        c_in = [sem(f"c_in{k}") for k in range(C_RING)]

        block = ctx.enter_context(nc.Block())

        def following(b, s):
            return (b, s + 1) if s + 1 < NG else (b + 1, 0)

        def prepares(prepare, b, s, n, last):
            nxt = following(b, s)
            if not (last and s == NG - 1):
                for stage, step in LATER_STAGES.items():
                    if step == n:
                        prepare(*nxt, stage)
            if not (last and s >= NG - 2):
                for stage, step in FIRST_STAGES.items():
                    if step == n:
                        prepare(*following(*nxt), stage)

        def batches(eng, body):
            body(0, True, False)
            with eng.Fori(1, BATCH - 1) as b:
                body(b, False, False)
            body(BATCH - 1, False, True)

        def wait_c_product(eng, b, s, n):
            if n in POOL_C[s]:
                eng.wait_ge(ch_pool, pool_c(b, s, n) + 1)
            else:
                eng.wait_ge(ch_vector, vector_c(b, s, n) + 1)

        def chunk_of(s):
            c = GROUPS[s][1]
            return slice(c * CHUNK, (c + 1) * CHUNK)

        def in_scan_order(ap, s):
            return ap if GROUPS[s][0] == FWD else ap[:, ::-1]

        def da_bank(n, a):
            return (DT * n + a) % DA_BANKS

        def first_x_bank(j):
            return (da_ps[:, 0, :], da_ps[:, 1, :], c_ps[:, 0, :], c_ps[:, 1, :])[j]

        def last_bank(j):
            return (c_ps[:, 0, :], c_ps[:, 1, :], y_ps[:, 0, :], y_ps[:, 1, :],
                    da_ps[:, 0, :], da_ps[:, 1, :], da_ps[:, 2, :], pre[:])[j]

        def last_column(s):
            return CHUNK - 1 if GROUPS[s][0] == FWD else 0

        @block.sync
        def _(sp):
            sp.dma_start(h_in[:], h_tiles[0]).then_inc(h_in_ready, 16)
            sp.dma_start(w_in_raw, w_in.rearrange("(q p) m -> p q m", p=P)).then_inc(w_in_in, 16)
            directions = ((conv_w_f, conv_b_f, wx_f, wdt_f, bdt_f, alog_f, d_f),
                          (conv_w_r, conv_b_r, wx_r, wdt_r, bdt_r, alog_r, d_r))

            def per_channel(tile, source):
                return sp.dma_start(tile, source.rearrange("(a p) -> p a", p=P), allow_slow_non_contiguous=True)

            def load_conv(g, loaded):
                cw, cb = directions[g][:2]
                sp.dma_start(conv_w[:, g], cw.rearrange("(a p) k -> p a k", p=P)).then_inc(loaded, 16)
                per_channel(conv_b[:, g], cb).then_inc(loaded, 16)

            def load_step_weights(g):
                wx, wdt = directions[g][2:4]
                sp.dma_start(wx_raw[0:32, g, :], wx[RANK:RANK + 32, :]).then_inc(weights_in, 16)
                sp.dma_start(wx_raw[32:64, g, :], wx[RANK:RANK + 32, :]).then_inc(weights_in, 16)
                sp.dma_start(wx_raw[64:128, g, :], wx[0:RANK, :]).then_inc(weights_in, 16)
                sp.dma_start(wdt_raw[:, g, :, RANK:], wdt.rearrange("(a p) r -> p a r", p=P)).then_inc(weights_in, 16)

            load_conv(FWD, conv_in)
            load_step_weights(FWD)
            load_step_weights(REV)
            sp.dma_start(w_out_raw, w_out).then_inc(weights_in, 16)
            for g in (FWD, REV):
                _, _, _, _, bd, al, d = directions[g]
                per_channel(bdt[:, g], bd).then_inc(dt_cols_in, 16)
                sp.dma_start(neg_a[:, g], al.rearrange("(a p) n -> p a n", p=P)).then_inc(dt_cols_in, 16)
                per_channel(d_col[:, g], d).then_inc(dt_cols_in, 16)
            load_conv(REV, cols_in)
            sp.dma_start(gamma_col[:], ln_gamma.rearrange("(p o) -> p o", o=1)).then_inc(cols_in, 16)
            sp.dma_start(beta_col[:], ln_beta.rearrange("(p o) -> p o", o=1)).then_inc(cols_in, 16)
            sp.dma_start(w_raw[:], w_ffn).then_inc(cols_in, 16)

            def tokens_of(b):
                return h_tiles[b] if isinstance(b, int) else h_tiles[bass.ds(b, 1)].rearrange("o p t m -> p (o t) m")

            def store_rows(b, s):
                sp.wait_ge(x_dbl_sb, NG * b + s + 1)
                sp.dma_start(bc_rows[s], x_dbl[0:2 * STATES, :]).then_inc(rows_stored, 16)

            def load_b(b, s, n):
                group = NG * b + s
                if not (isinstance(group, int) and group == 0 and n < RING):
                    sp.wait_ge(dbx_ready, STATES * group + n - RING + 1)
                sp.dma_start(b_ring[:, n % RING, :], bc_rows[s, n, :].partition_broadcast(P)).then_inc(b_in[n % RING], 16)

            def load_c(b, s, n):
                slot = pool_c(0, s, n) % C_RING
                if n == POOL_C[s][0]:
                    sp.wait_ge(rows_stored, 16 * (NG * b + s + 1))
                sp.dma_start(c_ring[:, slot, :],
                             bc_rows[s, STATES + n, :].partition_broadcast(P)).then_inc(c_in[slot], 16)

            def batch(b, first, last):
                for s in range(NG):
                    if s == 0 and not last:
                        sp.wait_ge(ht_ps, CHUNKS * (b + 1))
                        sp.dma_start(h_in[:], tokens_of(b + 1)).then_inc(h_in_ready, 16)
                    if s == 2:
                        if not first:
                            sp.wait_ge(resid_ready, CHUNKS * b)
                        sp.dma_start(h_res[:], tokens_of(b)).then_inc(h_res_ready, 16)
                    load_c(b, s, POOL_C[s][0])
                    for n in range(STATES):
                        load_b(b, s, n)
                        if n in POOL_C[s][1:]:
                            load_c(b, s, n)
                        if n == ROWS_AT and not (last and s == NG - 1):
                            store_rows(*following(b, s))

            store_rows(0, 0)
            batches(sp, batch)
            for c in range(BATCH):
                sp.wait_ge(final_ready, c + 1)
                tiles = slice(c * TILES // BATCH, (c + 1) * TILES // BATCH)
                sp.dma_start(out_tiles[:, tiles, :], z_last[:, tiles, :]).then_inc(stored, 16)
            sp.wait_ge(stored, 16 * BATCH)

        @block.gpsimd
        def _(pool):
            nc.gpsimd.memset(ident[:], 0.0).then_inc(ident_zero, 1)
            pool.wait_ge(ident_zero, 1)
            nc.gpsimd.affine_select(out=ident[:], in_=ident[:], compare_op=ALU.not_equal, fill=1.0, base=0,
                                    pattern=[[-1, P]], channel_multiplier=1).then_inc(ident_ready, 1)
            nc.gpsimd.memset(wdt_raw[:, :, :, 0:RANK], 0.0).then_inc(raw_zero, 1)
            nc.gpsimd.memset(x_pad[:, :, 0:PAD], 0.0).then_inc(pads_ready, 1)
            nc.gpsimd.memset(x_pad[:, :, PAD + SEQ:], 0.0).then_inc(pads_ready, 1)
            nc.gpsimd.memset(bc_parts[:], 0.0).then_inc(pads_ready, 1)
            nc.gpsimd.memset(above_one[:], 1.0 + 2.0 ** -23).then_inc(pads_ready, 1)
            nc.gpsimd.memset(minus_three_quarters[:], -0.75).then_inc(pads_ready, 1)
            nc.gpsimd.memset(half[:], -0.5).then_inc(half_ready, 1)
            pool.wait_ge(half_ready, 1)

            def times_b(b, s, n):
                group = NG * b + s
                if n == 0:
                    pool.wait_ge(dtx_ready, group + 1)
                pool.wait_ge(b_in[n % RING], 16 * (STATES // RING * group + n // RING + 1))
                if not (isinstance(group, int) and group == 0 and n < RING):
                    pool.wait_ge(scanned, DT * (STATES * group + n - RING + 1))
                nc.gpsimd.tensor_tensor(dbx[:, n % RING], dtx[:, s % 2],
                                        b_ring[:, n % RING, :].unsqueeze(1).to_broadcast([P, DT, CHUNK]),
                                        ALU.mult).then_inc(dbx_ready, 1)

            def times_c(b, s, n):
                group = NG * b + s
                pool.wait_ge(scanned, DT * (STATES * group + n + 1))
                slot = pool_c(0, s, n) % C_RING
                pool.wait_ge(c_in[slot], 16 * (NPC // C_RING * b + pool_c(0, s, n) // C_RING + 1))
                if not (isinstance(group, int) and group == 0 and n < RING):
                    pool.wait_ge(summed, STATES * group + n - RING + 1)
                nc.gpsimd.tensor_tensor(ch[:, n % RING], hs[:, n % RING],
                                        c_ring[:, slot, :].unsqueeze(1).to_broadcast([P, DT, CHUNK]),
                                        ALU.mult).then_inc(ch_pool, 1)

            def inverse_deviation(e, mv, mv_ready, rstd, rstd_ready, eps):
                pool.wait_ge(mv_ready, 2 * (e + 1))
                nc.gpsimd.tensor_tensor(rstd[:], mv[:, :, 1], half[:, 0:TT], ALU.pow).then_inc(rstd_ready, 1)

            def batch(b, first, last):
                for s in range(NG):
                    for n in range(STATES):
                        if first and s == 1 and n == 0:
                            pool.wait_ge(w_sum, 1)
                            nc.gpsimd.partition_all_reduce(tiny[:, 1:2], tiny[:, 0:1], P, REDUCE.add).then_inc(w_sum_all, 1)
                        if n - 1 in POOL_C[s]:
                            times_c(b, s, n - 1)
                        if n + B_AHEAD < STATES:
                            times_b(b, s, n + B_AHEAD)
                        elif not (last and s == NG - 1):
                            times_b(*following(b, s), n + B_AHEAD - STATES)
                        if s == NG - 1 or (s == 0 and not first):
                            e = 2 * b if s else 2 * b - 1
                            if n == CLOSING["deviation1"]:
                                inverse_deviation(e, mv1, mv1_ready, rstd1, rstd1_ready, LN1_EPS)
                            if n == CLOSING["deviation2"]:
                                inverse_deviation(e, mv2, mv2_ready, rstd2, rstd2_ready, LN2_EPS)

            for n in range(B_AHEAD):
                times_b(0, 0, n)
            batches(pool, batch)
            e = 2 * BATCH - 1
            inverse_deviation(e, mv1, mv1_ready, rstd1, rstd1_ready, LN1_EPS)
            inverse_deviation(e, mv2, mv2_ready, rstd2, rstd2_ready, LN2_EPS)
            pool.wait_ge(max_ready, 2 * BATCH + 1)
            nc.gpsimd.partition_all_reduce(tiny[:, 5:6], tiny[:, 4:5], P, REDUCE.max).then_inc(all_max, 1)
            for c in range(BATCH):
                pool.wait_ge(mv_last_ready, 2 * (c + 1))
                t = slice(c * TILES // BATCH, (c + 1) * TILES // BATCH)
                nc.gpsimd.tensor_tensor(rstd_last[:, t], mv_last[:, t, 1], half[:, t],
                                        ALU.pow).then_inc(rstd_last_ready, 1)

        @block.scalar
        def _(act):
            nc.scalar.preload_act_table_set(SILU)

            def copy_ht(b, c):
                act.wait_ge(ht_ps, CHUNKS * b + c + 1)
                bank = c_ps[:, c, :] if isinstance(b, int) and b == 0 else pre[:]
                nc.scalar.copy(h_t[:, c * CHUNK:(c + 1) * CHUNK], bank).then_inc(ht_sb, 1)

            def copy_x(b, j):
                c, a = divmod(j, DT)
                if j == 0 and not (isinstance(b, int) and b == 0):
                    act.wait_ge(conv, (TAPS - 1) * NG * b)
                act.wait_ge(x_ps, DT * CHUNKS * b + j + 1)
                bank = first_x_bank(j) if isinstance(b, int) and b == 0 else pre[:]
                nc.scalar.copy(x_pad[:, a, PAD + c * CHUNK:PAD + (c + 1) * CHUNK], bank).then_inc(x_sb, 1)

            def copy_z(b, j):
                a, c = divmod(j, CHUNKS)
                if j == 0 and not (isinstance(b, int) and b == 0):
                    act.wait_ge(g_ready, CHUNKS * b)
                act.wait_ge(z_ps, DT * CHUNKS * b + j + 1)
                nc.scalar.copy(silu_z[:, a, c * CHUNK:(c + 1) * CHUNK], pre[:]).then_inc(z_raw, 1)

            def prepare(b, s, stage):
                q = NG * b + s
                g, c = GROUPS[s]
                par = s % 2
                zero = isinstance(q, int) and q == 0
                if stage == "tap0":
                    act.wait_ge(x_sb, DT * (CHUNKS * b + (1 if s == 0 else CHUNKS)))
                    if zero:
                        act.wait_ge(pads_ready, 5)
                    if not (isinstance(q, int) and q < 2):
                        act.wait_ge(summed, STATES * (q - 2) + 1)
                        act.wait_ge(dtx_ready, q - 1)
                    at = c * CHUNK + (0 if g == FWD else 2 * PAD)
                    nc.scalar.activation(xs[:, par, 1, :], x_pad[:, 1, at:at + CHUNK], ACT.Identity,
                                         scale=conv_w[:, g, 1, 0:1], bias=conv_b[:, g, 1:2]).then_inc(tap0, 1)
                if stage == "take conv":
                    act.wait_ge(conv_ps, q + 1)
                    nc.scalar.activation(xs[:, par, 0, :], pre[:], ACT.Identity, bias=conv_b[:, g, 0:1]).then_inc(conv_sb, 1)
                if stage == "silu":
                    act.wait_ge(conv_sb, q + 1)
                    act.wait_ge(conv, (TAPS - 1) * (q + 1))
                    nc.scalar.activation(xs[:, par], xs[:, par], ACT.Silu).then_inc(xs_ready, 1)
                if stage == "copy x_dbl":
                    act.wait_ge(x_dbl_ps, q + 1)
                    if not zero:
                        act.wait_ge(u_ps, 2 * q)
                        act.wait_ge(bc_rest_ready, q)
                        act.wait_ge(rows_stored, 16 * q)
                    nc.scalar.copy(x_dbl[:], pre[:]).then_inc(x_dbl_sb, 1)
                    if not (isinstance(q, int) and q < 2):
                        act.wait_ge(c_ps_ready, vector_c(b, s - 1) if s else vector_c(b - 1, NG - 1))
                    nc.scalar.copy(bc_parts[0:64, par], pre[0:64, :]).then_inc(bc_hi, 1)
                if stage == "middle":
                    act.wait_ge(bc_rest_ready, q + 1)
                    nc.scalar.copy(bc_parts[32:64, par], bc_rest[32:64, :]).then_inc(bc_mid, 1)
                if stage in ("take u0", "take u1"):
                    a = int(stage[-1])
                    act.wait_ge(u_ps, 2 * q + a + 1)
                    if not zero and a == 0:
                        act.wait_ge(dt_ready, q)
                    u = first_x_bank(3) if zero and a else pre[:]
                    nc.scalar.activation(sp_e[:, a], u, ACT.Abs, bias=bdt[:, g, a:a + 1]).then_inc(u_taken, 1)
                    nc.scalar.activation(sp_r[:, a], u, ACT.Relu, bias=bdt[:, g, a:a + 1]).then_inc(u_taken, 1)
                if stage == "exp":
                    act.wait_ge(u_taken, 4 * (q + 1))
                    nc.scalar.activation(sp_e[:], sp_e[:], ACT.Exp, scale=-1.0).then_inc(sp_e_ready, 1)
                if stage == "square":
                    act.wait_ge(sp_e_ready, q + 1)
                    nc.scalar.activation(sp_s[:], sp_e[:], ACT.Square, bias=minus_three_quarters[:]).then_inc(sp_square, 1)
                if stage == "ln":
                    nc.scalar.activation(sp_l[:], sp_e[:], ACT.Ln, bias=above_one[:]).then_inc(sp_l_ready, 1)

            def silu_of_z(b, c):
                act.wait_ge(z_raw, DT * CHUNKS * (b + 1))
                part = silu_z[:, :, c * CHUNK:(c + 1) * CHUNK]
                nc.scalar.activation(part, part, ACT.Silu).then_inc(silu_z_ready, 1)

            def keep_state(b, s, n):
                act.wait_ge(scanned, DT * (STATES * (NG * b + s) + n + 1))
                nc.scalar.copy(carry[:, :, n:n + 1],
                               hs[:, n % RING, :, last_column(s):last_column(s) + 1]).then_inc(carried, 1)

            def normalise(b_e, h_e):
                e = 2 * b_e + h_e
                act.wait_ge(bias1_ready, e + 1)
                for j in range(TT):
                    nc.scalar.activation(xn[:, j, :], resid[:, j, :], ACT.Identity, scale=rstd1[:, j:j + 1],
                                         bias=bias1[:, j:j + 1]).then_inc(x1_ready, 1)

            def normalise_again(b_e, h_e):
                e = 2 * b_e + h_e
                act.wait_ge(x1_kept, e + 1)
                act.wait_ge(bias2_ready, e + 1)
                for j in range(TT):
                    nc.scalar.activation(xn[:, j, :], xn[:, j, :], ACT.Identity, scale=rstd2[:, j:j + 1],
                                         bias=bias2[:, j:j + 1]).then_inc(xn_ready, 1)

            def keep_x1(b_e, h_e):
                e = 2 * b_e + h_e
                act.wait_ge(x1_ready, TT * (e + 1))
                tile = (SEQ // P) * b_e + (1 - h_e) * TT
                dst = x1[:, tile:tile + TT, :] if isinstance(tile, int) else x1[:, bass.ds(tile, TT), :]
                nc.scalar.copy(dst, xn[:]).then_inc(x1_kept, 1)

            def norm_out(b_e, h_e):
                e = 2 * b_e + h_e
                act.wait_ge(xn_ps, e + 1)
                col = (SEQ * b_e + (1 - h_e) * CHUNK)
                dst = xn_t[:, col:col + CHUNK] if isinstance(col, int) else xn_t[:, bass.ds(col, CHUNK)]
                nc.scalar.activation(dst, pre[:], ACT.Identity,
                                     scale=gamma_col[:], bias=beta_col[:]).then_inc(xn_sb, 1)

            def batch(b, first, last):
                for s in range(NG):
                    group = NG * b + s
                    g, c = GROUPS[s]
                    if not first and s == 0:
                        nc.scalar.preload_act_table_set(EXP_LN)
                    for n in range(STATES):
                        if n == 0:
                            act.wait_ge(dt_ready, group + 1)
                        first_half, last_half = DT * n, DT * n + 1
                        if n == FIRST_STAGES["silu"]:
                            last_half += EXPS_AHEAD
                        if n == FIRST_STAGES["silu"] + 1:
                            first_half += EXPS_AHEAD
                        for half in range(first_half, last_half + 1):
                            state, a = divmod(half, DT)
                            if half >= DA_BANKS:
                                act.wait_ge(scanned, DT * STATES * group + half - DA_BANKS + 1)
                            elif not (first and s == 0):
                                same_bank = max(k for k in range(DT * STATES) if k % DA_BANKS == half)
                                act.wait_ge(scanned, DT * STATES * (group - 1) + same_bank + 1)
                            nc.scalar.activation(da_ps[:, half % DA_BANKS, :], dt[:, s % 2, a, :], ACT.Exp,
                                                 scale=neg_a[:, g, a, state:state + 1]).then_inc(da_ready, 1)
                        if n >= 2 and s in (0, 2):
                            keep_state(b, s, n - 2)
                        elif n < 2 and s in (1, 3):
                            keep_state(b, s - 1, n - 2 + STATES)
                        if n == CLOSING["save"] and s == 1:
                            act.wait_ge(summed, STATES * group)
                            nc.scalar.copy(y_fwd[:], y_ps[:]).then_inc(y_saved, 1)
                        for j in range(DT * CHUNKS):
                            if n == PROJECTIONS_READ[f"z{j}"] and s == j // 2:
                                copy_z(b, j)
                        if s == 1 and not last:
                            for c in range(CHUNKS):
                                if n == PROJECTIONS_READ[f"h{c}"]:
                                    copy_ht(b + 1, c)
                        if s == 2 and not last:
                            for j in range(DT * CHUNKS):
                                if n == PROJECTIONS_READ[f"x{j}"]:
                                    copy_x(b + 1, j)
                        if s == NG - 1 or (s == 0 and not first):
                            of, h_e = (b, 0) if s else (b - 1, 1)
                            if n == CLOSING["scale1"]:
                                normalise(of, h_e)
                            if n == CLOSING["scale2"]:
                                normalise_again(of, h_e)
                            if n == CLOSING["keep"]:
                                keep_x1(of, h_e)
                            if n == CLOSING["affine"]:
                                norm_out(of, h_e)
                        if n == CONVOLVE[s] + 2 and not (last and s >= NG - 2):
                            prepare(*following(*following(b, s)), "take conv")
                        prepares(prepare, b, s, n, last)
                        if n == FIRST_STAGES["silu"]:
                            if s in (1, 2):
                                silu_of_z(b, 2 - s)
                            nc.scalar.preload_act_table_set(EXP_LN)

            copy_ht(0, 0)
            copy_x(0, 0)
            copy_x(0, 1)
            act.wait_ge(conv_in, 16 * 2)
            prepare(0, 0, "tap0")
            prepare(0, 0, "take conv")
            copy_ht(0, 1)
            prepare(0, 0, "silu")
            nc.scalar.preload_act_table_set(EXP_LN)
            copy_x(0, 2)
            copy_x(0, 3)
            prepare(0, 1, "tap0")
            act.wait_ge(dt_cols_in, 16 * 6)
            for stage in LATER_STAGES:
                prepare(0, 0, stage)
            nc.scalar.activation(neg_a[:], neg_a[:], ACT.Exp).then_inc(a_exp, 1)
            prepare(0, 1, "take conv")
            prepare(0, 1, "silu")
            nc.scalar.preload_act_table_set(EXP_LN)
            act.wait_ge(a_ready, 1)
            act.wait_ge(cols_in, 16 * 5)
            batches(act, batch)
            normalise(BATCH - 1, 1)
            keep_x1(BATCH - 1, 1)
            normalise_again(BATCH - 1, 1)
            norm_out(BATCH - 1, 1)
            per = TILES // BATCH
            for c in range(BATCH):
                act.wait_ge(bias_last_ready, c + 1)
                for m in range(per * c, per * (c + 1)):
                    ins = nc.scalar.activation(z_last[:, m, :], z_last[:, m, :], ACT.Identity,
                                               scale=rstd_last[:, m:m + 1], bias=bias_last[:, m:m + 1])
                ins.then_inc(final_ready, 1)

        @block.vector
        def _(dve):
            small = [0]

            def chained(ins):
                small[0] += 1
                ins.then_inc(small_dve, 1)
                dve.wait_ge(small_dve, small[0])

            dve.wait_ge(ident_ready, 1)
            chained(nc.vector.tensor_tensor(xn[:, 0, 0:32], ident[:, 0:32], ident[:, 32:64], ALU.add))
            chained(nc.vector.tensor_tensor(xn[:, 0, 0:32], xn[:, 0, 0:32], ident[:, 64:96], ALU.add))
            nc.vector.tensor_copy(select[:], xn[:, 0, STATES:2 * STATES].unsqueeze(2).to_broadcast([P, STATES, P])
                                  ).then_inc(select_ready, 1)
            dve.wait_ge(weights_ps, 1)
            nc.vector.tensor_copy(w_in_t[:], y_ps[:, 0, :]).then_inc(weights_sb, 1)

            def make_diag_conv(g):
                for k in range(TAPS):
                    nc.vector.tensor_scalar(diag_conv[:, g, k, :], ident[:], conv_w[:, g, 0, k:k + 1], None,
                                            ALU.mult).then_inc(diag_conv_ready, 1)

            dve.wait_ge(conv_in, 16 * 2)
            make_diag_conv(FWD)

            def copy_weights():
                dve.wait_ge(weights_ps, 4)
                nc.vector.tensor_copy(w_mix_t[:].rearrange("p a m -> p (a m)"), y_ps[:, 1, :]).then_inc(weights_sb, 1)
                nc.vector.tensor_copy(wdt_t[:].rearrange("p g a m -> p (g a m)"), da_ps[:, 2, :]).then_inc(weights_sb, 1)
                nc.vector.tensor_copy(wx_rev_t[:].rearrange("p a m -> p (a m)"), pre[:, 0:DT * P]).then_inc(weights_sb, 1)

            def constants():
                dve.wait_ge(a_exp, 1)
                nc.vector.tensor_scalar(neg_a[:], neg_a[:], -1.0, None, ALU.mult).then_inc(a_ready, 1)
                for g in range(2):
                    for a in range(DT):
                        nc.vector.tensor_scalar(diag_d[:, g, a, :], ident[:], d_col[:, g, a:a + 1], None,
                                                ALU.mult).then_inc(diag_ready, 1)

            def quantise_weight():
                dve.wait_ge(w_sum_all, 1)
                chained(nc.vector.tensor_scalar(tiny[:, 2:3], tiny[:, 1:2], 1.0 / (P * P), None, ALU.mult))
                chained(nc.vector.tensor_scalar(tiny[:, 3:4], tiny[:, 2:3], QUANT_EPS, None, ALU.add))
                chained(nc.vector.reciprocal(tiny[:, 3:4], tiny[:, 3:4]))
                chained(nc.vector.tensor_scalar(w_q[:], w_raw[:], tiny[:, 3:4], ROUND, ALU.mult, ALU.add))
                chained(nc.vector.tensor_scalar(w_q[:], w_q[:], ROUND, 1.0, ALU.subtract, ALU.min))
                nc.vector.tensor_scalar(w_q[:], w_q[:], -1.0, None, ALU.max).then_inc(wq_ready, 1)

            def prepare(b, s, stage):
                q = NG * b + s
                g, c = GROUPS[s]
                par = s % 2
                if stage in ("tap1", "tap2", "tap3"):
                    k = int(stage[-1])
                    if k == 1:
                        dve.wait_ge(tap0, q + 1)
                    else:
                        dve.wait_ge(conv, (TAPS - 1) * q + k - 1)
                    at = c * CHUNK + (k if g == FWD else 2 * PAD - k)
                    nc.vector.scalar_tensor_tensor(xs[:, par, 1, :], x_pad[:, 1, at:at + CHUNK],
                                                   conv_w[:, g, 1, k:k + 1], xs[:, par, 1, :],
                                                   ALU.mult, ALU.add).then_inc(conv, 1)
                if stage == "rest":
                    dve.wait_ge(x_dbl_sb, q + 1)
                    dve.wait_ge(bc_hi, q + 1)
                    nc.vector.tensor_tensor(bc_rest[:], x_dbl[0:64, :], bc_parts[0:64, par],
                                            ALU.subtract).then_inc(bc_rest_ready, 1)
                if stage == "third":
                    dve.wait_ge(bc_mid, q + 1)
                    nc.vector.tensor_tensor(bc_parts[64:96, par], bc_rest[32:64, :], bc_parts[32:64, par],
                                            ALU.subtract).then_inc(bc_ready, 1)
                if stage == "series":
                    dve.wait_ge(sp_square, q + 1)
                    nc.vector.scalar_tensor_tensor(sp_s[:], sp_s[:], 39.0 / 16.0, sp_e[:],
                                                   ALU.add, ALU.mult).then_inc(sp_cube, 1)
                if stage == "min":
                    dve.wait_ge(sp_cube, q + 1)
                    dve.wait_ge(sp_l_ready, q + 1)
                    nc.vector.scalar_tensor_tensor(sp_s[:], sp_l[:], 3.0, sp_s[:],
                                                   ALU.mult, ALU.min).then_inc(sp_min, 1)
                if stage == "dt":
                    dve.wait_ge(sp_min, q + 1)
                    if not (isinstance(q, int) and q < 2):
                        dve.wait_ge(da_ready, DT * STATES * (q - 1))
                    nc.vector.scalar_tensor_tensor(dt[:, par], sp_s[:], 1.0 / 3.0, sp_r[:],
                                                   ALU.mult, ALU.add).then_inc(dt_ready, 1)
                if stage == "dtx":
                    dve.wait_ge(dt_ready, q + 1)
                    dve.wait_ge(xs_ready, q + 1)
                    if not (isinstance(q, int) and q < 2):
                        dve.wait_ge(dbx_ready, STATES * (q - 1))
                    nc.vector.tensor_tensor(dtx[:, par], dt[:, par], xs[:, par], ALU.mult).then_inc(dtx_ready, 1)

            def times_c(b, s, n):
                group = NG * b + s
                dve.wait_ge(c_ps_ready, vector_c(b, s, n) + 1)
                dve.wait_ge(scanned, DT * (STATES * group + n + 1))
                if not (isinstance(group, int) and group == 0 and n < RING):
                    dve.wait_ge(summed, STATES * group + n - RING + 1)
                nc.vector.tensor_tensor(ch[:, n % RING], hs[:, n % RING],
                                        c_ps[:, vector_c(0, s, n) % C_BANKS, :].unsqueeze(1).to_broadcast([P, DT, CHUNK]),
                                        ALU.mult).then_inc(ch_vector, 1)

            def gate(b, s):
                e = 2 * b + (1 if s == 3 else 0)
                dve.wait_ge(summed, STATES * (NG * b + s + 1))
                dve.wait_ge(silu_z_ready, e + 1)
                if not (isinstance(e, int) and e == 0):
                    dve.wait_ge(o_ps, e)
                nc.vector.tensor_tensor(gated[:], y_ps[:], silu_z[:, :, chunk_of(s)], ALU.mult).then_inc(g_ready, 1)

            def statistics(source):
                for j in range(TT):
                    nc.vector.bn_stats(stats[:, j, :], source[:, j, :]).then_inc(stats_ready, 1)

            def statistics_wait(e, layer):
                dve.wait_ge(stats_ready, 2 * TT * e + TT * (layer + 1))

            def aggregate(mv, mv_ready):
                for j in range(TT):
                    ins = nc.vector.bn_aggr(mv[:, j, :], stats[:, j, :])
                ins.then_inc(mv_ready, 1)

            def add_eps(e, mv, mv_ready, eps):
                dve.wait_ge(mv_ready, 2 * e + 1)
                nc.vector.tensor_scalar(mv[:, :, 1], mv[:, :, 1], eps, None, ALU.add).then_inc(mv_ready, 1)

            def norm_first(b, h_e, n):
                e = 2 * b + h_e
                tile0 = (1 - h_e) * TT
                if n == CLOSING["residual"]:
                    dve.wait_ge(h_res_ready, 16 * (b + 1))
                    dve.wait_ge(o_ps, e + 1)
                    nc.vector.tensor_tensor(resid[:], pre[:].rearrange("p (t m) -> p t m", t=TT),
                                            h_res[:, tile0:tile0 + TT, :], ALU.add).then_inc(resid_ready, 1)
                if n == CLOSING["mean1"]:
                    aggregate(mv1, mv1_ready)
                if n == CLOSING["bias1"]:
                    dve.wait_ge(rstd1_ready, e + 1)
                    nc.vector.scalar_tensor_tensor(bias1[:], mv1[:, :, 0], -1.0, rstd1[:],
                                                   ALU.mult, ALU.mult).then_inc(bias1_ready, 1)
                if n == CLOSING["mean2"]:
                    aggregate(mv2, mv2_ready)
                if n == CLOSING["bias2"]:
                    dve.wait_ge(rstd2_ready, e + 1)
                    nc.vector.scalar_tensor_tensor(bias2[:], mv2[:, :, 0], -1.0, rstd2[:],
                                                   ALU.mult, ALU.mult).then_inc(bias2_ready, 1)

            def norm_second(b, h_e, n):
                e = 2 * b + h_e
                if n == CLOSING["residual"]:
                    dve.wait_ge(resid_ready, e + 1)
                    statistics(resid)
                if n == CLOSING["mean1"]:
                    add_eps(e, mv1, mv1_ready, LN1_EPS)
                if n == CLOSING["scale1"]:
                    dve.wait_ge(x1_ready, TT * (e + 1))
                    statistics(xn)
                if n == CLOSING["mean2"]:
                    add_eps(e, mv2, mv2_ready, LN2_EPS)

            def largest(b, h_e):
                e = 2 * b + h_e
                dve.wait_ge(xn_sb, e + 1)
                col = SEQ * b + (1 - h_e) * CHUNK
                slot = part_max[:, e:e + 1] if isinstance(e, int) else part_max[:, bass.ds(e, 1)]
                src = xn_t[:, col:col + CHUNK] if isinstance(col, int) else xn_t[:, bass.ds(col, CHUNK)]
                nc.vector.tensor_reduce(slot, src, X, ALU.max, apply_absolute_value=True).then_inc(max_ready, 1)

            def batch(b, first, last):
                for s in range(NG):
                    group = NG * b + s
                    g, c = GROUPS[s]
                    starts = s in (0, 2)
                    for n in range(STATES):
                        for layer in range(2):
                            if n == CLOSING[f"mean{layer + 1}"]:
                                if s == NG - 1:
                                    statistics_wait(2 * b, layer)
                                if s == 0 and not first:
                                    statistics_wait(2 * b - 1, layer)
                        for a in range(DT):
                            idx = STATES * group + n
                            dve.wait_ge(da_ready, DT * idx + a + 1)
                            if a == 0:
                                dve.wait_ge(dbx_ready, idx + 1)
                                if n >= RING:
                                    wait_c_product(dve, b, s, n - RING)
                                elif not (first and s == 0):
                                    pb_, ps_ = (b, s - 1) if s else (b - 1, NG - 1)
                                    wait_c_product(dve, pb_, ps_, n - RING + STATES)
                                if n >= RING and starts:
                                    dve.wait_ge(carried, STATES * (2 * b + s // 2) + n - RING + 1)
                                elif n < RING and not starts:
                                    dve.wait_ge(carried, STATES * (2 * b + s // 2) + n - RING + STATES + 1)
                            if starts:
                                initial = 0.0
                            else:
                                initial = carry[:, a, n:n + 1]
                                if a == 0 and n >= RING:
                                    dve.wait_ge(carried, STATES * (2 * b + s // 2) + n + 1)
                            nc.vector.tensor_tensor_scan(in_scan_order(hs[:, n % RING, a, :], s),
                                                         in_scan_order(da_ps[:, da_bank(n, a), :], s),
                                                         in_scan_order(dbx[:, n % RING, a, :], s),
                                                         initial, ALU.mult, ALU.add).then_inc(scanned, 1)
                        if s == NG - 1:
                            norm_first(b, 0, n)
                        if s == 0 and not first:
                            norm_first(b - 1, 1, n)
                        if n:
                            prev = (b, s, n - 1)
                        else:
                            prev = (b, s - 1, STATES - 1) if s else (b - 1, NG - 1, STATES - 1)
                        if not (first and s == 0 and n == 0):
                            if prev[2] not in POOL_C[prev[1]]:
                                times_c(*prev)
                        if n == CLOSING["gate"] and s == 3:
                            gate(b, 2)
                        if n == CLOSING["gate"] and s == 0 and not first:
                            gate(b - 1, 3)
                        if s == NG - 1:
                            norm_second(b, 0, n)
                        if s == 0 and not first:
                            norm_second(b - 1, 1, n)
                        if n == CLOSING["largest"] and s == 3:
                            largest(b, 0)
                        if n == CLOSING["largest"] and s == 0 and not first:
                            largest(b - 1, 1)
                        prepares(prepare, b, s, n, last)
                        if first and s == 1 and n == 4:
                            quantise_weight()

            for stage in ("tap1", "tap2", "tap3"):
                prepare(0, 0, stage)
            copy_weights()
            prepare(0, 1, "tap1")
            prepare(0, 0, "rest")
            prepare(0, 1, "tap2")
            prepare(0, 0, "third")
            prepare(0, 1, "tap3")
            for stage in ("series", "min", "dt", "dtx"):
                prepare(0, 0, stage)
            constants()
            dve.wait_ge(cols_in, 16 * 5)
            make_diag_conv(REV)
            nc.vector.tensor_reduce(tiny[:, 0:1], w_raw[:], X, ALU.add, apply_absolute_value=True).then_inc(w_sum, 1)
            batches(dve, batch)
            times_c(BATCH - 1, NG - 1, STATES - 1)
            gate(BATCH - 1, 3)
            for n in range(STATES):
                for layer in range(2):
                    if n == CLOSING[f"mean{layer + 1}"]:
                        statistics_wait(2 * BATCH - 1, layer)
                norm_first(BATCH - 1, 1, n)
                norm_second(BATCH - 1, 1, n)
            largest(BATCH - 1, 1)
            gamma, inverse, scale_in, scale_out, scale, limit, minus_limit = (tiny[:, k:k + 1] for k in range(5, 12))
            dve.wait_ge(max_ready, 2 * BATCH)
            nc.vector.tensor_reduce(tiny[:, 4:5], part_max[:], X, ALU.max).then_inc(max_ready, 1)
            dve.wait_ge(all_max, 1)
            nc.vector.tensor_scalar(limit, gamma, (QB - QUANT_EPS) / QB, None, ALU.mult).then_inc(small_dve, 1)
            small[0] += 1
            chained(nc.vector.tensor_scalar(minus_limit, gamma, -(QB - QUANT_EPS) / QB, None, ALU.mult))

            def clip(c):
                t = slice(c * CHUNK, (c + 1) * CHUNK)
                nc.vector.tensor_scalar(xn_t[:, t], xn_t[:, t], limit, minus_limit, ALU.min, ALU.max).then_inc(clipped, 1)

            clip(0)
            clip(1)
            chained(nc.vector.reciprocal(inverse, gamma))
            clip(2)
            chained(nc.vector.tensor_scalar(scale_in, inverse, QB, None, ALU.mult))
            clip(3)
            chained(nc.vector.tensor_scalar(scale_out, gamma, tiny[:, 2:3], 1.0 / QB, ALU.mult, ALU.mult))
            clip(4)
            chained(nc.vector.tensor_tensor(scale, scale_in, scale_out, ALU.mult))
            for c in range(5, 2 * BATCH):
                clip(c)
            per = TILES // BATCH

            def last_sum(c):
                t0 = c * per
                for i in range(2):
                    j = 2 * c + i
                    dve.wait_ge(out_ps, j + 1)
                    t = slice(j * TT, (j + 1) * TT)
                    nc.vector.scalar_tensor_tensor(z_last[:, t, :].rearrange("p t m -> p (t m)"), last_bank(j),
                                                   scale, x1[:, t, :].rearrange("p t m -> p (t m)"),
                                                   ALU.mult, ALU.add).then_inc(z_ready, 1)
                for i in range(2):
                    j = 2 * c + i
                    dve.wait_ge(z_ready, j + 1)
                    for m in range(TT):
                        nc.vector.bn_stats(stats_last[:, j * TT + m, :], z_last[:, j * TT + m, :]).then_inc(stats_ready, 1)
                dve.wait_ge(stats_ready, 2 * TT * 2 * BATCH + per * (c + 1))
                for m in range(per):
                    ins = nc.vector.bn_aggr(mv_last[:, t0 + m, :], stats_last[:, t0 + m, :])
                ins.then_inc(mv_last_ready, 1)
                dve.wait_ge(mv_last_ready, 2 * c + 1)
                nc.vector.tensor_scalar(mv_last[:, t0:t0 + per, 1], mv_last[:, t0:t0 + per, 1], LN1_EPS, None,
                                        ALU.add).then_inc(mv_last_ready, 1)

            def last_bias(c):
                t = slice(c * per, (c + 1) * per)
                dve.wait_ge(rstd_last_ready, c + 1)
                nc.vector.scalar_tensor_tensor(bias_last[:, t], mv_last[:, t, 0], -1.0, rstd_last[:, t],
                                               ALU.mult, ALU.mult).then_inc(bias_last_ready, 1)

            for c in range(BATCH):
                last_sum(c)
                if c:
                    last_bias(c - 1)
            last_bias(BATCH - 1)

        @block.tensor
        def _(pe):
            pe.wait_ge(ident_ready, 1)

            def transpose_w_in():
                pe.wait_ge(w_in_in, 16)
                for q in range(4):
                    ins = nc.tensor.transpose(y_ps[:, 0, q * P:(q + 1) * P], w_in_raw[:, q, :], ident[:])
                ins.then_inc(weights_ps, 1)

            def transpose_weights():
                pe.wait_ge(weights_in, 16 * 9)
                pe.wait_ge(raw_zero, 1)
                for a in range(DT):
                    nc.tensor.transpose(y_ps[:, 1, a * P:(a + 1) * P], w_out_raw[:, a * P:(a + 1) * P], ident[:])
                    ins = nc.tensor.transpose(y_ps[:, 1, (2 + a) * P:(3 + a) * P], wx_raw[:, 0, a * P:(a + 1) * P], ident[:])
                ins.then_inc(weights_ps, 1)
                for g in range(2):
                    for a in range(DT):
                        k = DT * g + a
                        ins = nc.tensor.transpose(da_ps[:, 2, k * P:(k + 1) * P], wdt_raw[:, g, a, :], ident[:])
                ins.then_inc(weights_ps, 1)
                pe.wait_ge(conv_sb, 1)
                for a in range(DT):
                    ins = nc.tensor.transpose(pre[:, a * P:(a + 1) * P], wx_raw[:, 1, a * P:(a + 1) * P], ident[:])
                ins.then_inc(weights_ps, 1)

            def wx_half(g, a):
                return w_mix_t[:, 2 + a, :] if g == FWD else wx_rev_t[:, a, :]

            def transpose_h(b, c):
                if c == 0:
                    pe.wait_ge(h_in_ready, 16 * (b + 1))
                    if not (isinstance(b, int) and b == 0):
                        pe.wait_ge(z_raw, DT * CHUNKS * b)
                elif not (isinstance(b, int) and b == 0):
                    pe.wait_ge(ht_sb, CHUNKS * b + c)
                bank = c_ps[:, c, :] if isinstance(b, int) and b == 0 else pre[:]
                for t in range(TT):
                    ins = nc.tensor.transpose(bank[:, t * P:(t + 1) * P], h_in[:, c * TT + t, :], ident[:])
                ins.then_inc(ht_ps, 1)

            def project_x(b, j):
                c, a = divmod(j, DT)
                bank = pre[:]
                if isinstance(b, int) and b == 0:
                    pe.wait_ge(ht_sb, c + 1)
                    bank = first_x_bank(j)
                elif j == 0:
                    pe.wait_ge(ht_sb, CHUNKS * (b + 1))
                    pe.wait_ge(u_taken, 4 * NG * b)
                else:
                    pe.wait_ge(x_sb, DT * CHUNKS * b + j)
                nc.tensor.matmul(bank, w_in_t[:, a * P:(a + 1) * P], h_t[:, c * CHUNK:(c + 1) * CHUNK],
                                 start=True, stop=True).then_inc(x_ps, 1)

            def project_z(b, j, first=False):
                a, c = divmod(j, CHUNKS)
                if j == 0 and first:
                    pe.wait_ge(u_taken, 4 * 2)
                elif j == 0:
                    pe.wait_ge(resid_ready, CHUNKS * b)
                elif j == 2:
                    pe.wait_ge(u_taken, 4 * (NG * b + 3))
                else:
                    pe.wait_ge(z_raw, DT * CHUNKS * b + j)
                nc.tensor.matmul(pre[:], w_in_t[:, INNER + a * P:INNER + (a + 1) * P],
                                 h_t[:, c * CHUNK:(c + 1) * CHUNK], start=True, stop=True).then_inc(z_ps, 1)

            def convolve(b, s, pre_before):
                g, c = GROUPS[s]
                q = NG * b + s
                pe.wait_ge(x_sb, DT * (CHUNKS * b + (1 if s == 0 else CHUNKS)))
                pe.wait_ge(diag_conv_ready, TAPS * (g + 1))
                if pre_before:
                    pe.wait_ge(*pre_before)
                for k in range(TAPS):
                    at = c * CHUNK + (k if g == FWD else 2 * PAD - k)
                    ins = nc.tensor.matmul(pre[:], diag_conv[:, g, k, :], x_pad[:, 0, at:at + CHUNK],
                                           start=k == 0, stop=k == TAPS - 1)
                ins.then_inc(conv_ps, 1)

            def make_x_dbl(b, s, pre_before=None):
                g, c = GROUPS[s]
                pe.wait_ge(xs_ready, NG * b + s + 1)
                if pre_before:
                    pe.wait_ge(*pre_before)
                for a in range(DT):
                    ins = nc.tensor.matmul(pre[:], wx_half(g, a), xs[:, s % 2, a, :], start=a == 0, stop=a == DT - 1)
                ins.then_inc(x_dbl_ps, 1)

            def make_u(b, s, a):
                q = NG * b + s
                bank = pre[:]
                if a == 0:
                    pe.wait_ge(x_dbl_sb, q + 1)
                    pe.wait_ge(bc_hi, q + 1)
                elif isinstance(q, int) and q == 0:
                    bank = first_x_bank(3)
                else:
                    pe.wait_ge(u_taken, 4 * q + 2)
                nc.tensor.matmul(bank, wdt_t[:, GROUPS[s][0], a, :], x_dbl[:], start=True, stop=True).then_inc(u_ps, 1)

            def broadcast_c(b, s, n):
                group, k = NG * b + s, vector_c(0, s, n)
                if n == 0:
                    pe.wait_ge(bc_ready, group + 1)
                if not (isinstance(b, int) and b == 0 and k < C_BANKS):
                    pe.wait_ge(ch_vector, NVC * b + k - C_BANKS + 1)
                nc.tensor.matmul(c_ps[:, k % C_BANKS, :], select[:, n, :], bc_parts[:, s % 2],
                                 start=True, stop=True).then_inc(c_ps_ready, 1)

            def add_state(b, s, n):
                wait_c_product(pe, b, s, n)
                for a in range(DT):
                    ins = nc.tensor.matmul(y_ps[:, a, :], ident[:], ch[:, n % RING, a, :], start=False,
                                           stop=n == STATES - 1 and s != 1)
                ins.then_inc(summed, 1)

            def start_sum(b, s, first):
                g, c = GROUPS[s]
                if s == 0 and first:
                    pe.wait_ge(weights_sb, 2)
                    pe.wait_ge(diag_ready, 4)
                elif s == 0:
                    pe.wait_ge(g_ready, CHUNKS * b)
                elif s == 1:
                    pe.wait_ge(y_saved, b + 1)
                elif s == 3:
                    pe.wait_ge(g_ready, CHUNKS * b + 1)
                for a in range(DT):
                    nc.tensor.matmul(y_ps[:, a, :], diag_d[:, g, a, :], xs[:, s % 2, a, :], start=s != 2, stop=False)
                    if s == 3:
                        nc.tensor.matmul(y_ps[:, a, :], ident[:], y_fwd[:, a, :], start=False, stop=False)

            def output_product(b, h_e, last):
                e = 2 * b + h_e
                pe.wait_ge(g_ready, e + 1)
                if h_e == 0 and last:
                    pe.wait_ge(u_taken, 4 * NG * BATCH)
                elif h_e == 0:
                    pe.wait_ge(u_taken, 4 * (NG * (b + 1) + 1))
                elif last:
                    pe.wait_ge(xn_sb, e)
                else:
                    pe.wait_ge(u_taken, 4 * (NG * (b + 1) + 2))
                for t in range(TT):
                    for a in range(DT):
                        ins = nc.tensor.matmul(pre[:, t * P:(t + 1) * P], gated[:, a, t * P:(t + 1) * P],
                                               w_mix_t[:, a, :], start=a == 0, stop=a == DT - 1)
                ins.then_inc(o_ps, 1)

            def transpose_norm(b, h_e):
                e = 2 * b + h_e
                pe.wait_ge(xn_ready, TT * (e + 1))
                if isinstance(b, int) and b == BATCH - 1:
                    pe.wait_ge(resid_ready, e + 1)
                elif h_e == 0:
                    pe.wait_ge(conv_sb, NG * (b + 1) + 2)
                else:
                    pe.wait_ge(conv_sb, NG * (b + 1) + 3)
                for t in range(TT):
                    ins = nc.tensor.transpose(pre[:, t * P:(t + 1) * P], xn[:, t, :], ident[:])
                ins.then_inc(xn_ps, 1)

            def batch(b, first, last):
                before_conv = ((z_raw, DT * CHUNKS * b + 2),
                               (ht_sb, CHUNKS * (b + 2)) if not last else (z_raw, DT * CHUNKS * (b + 1)),
                               (x_sb, DT * CHUNKS * (b + 2)), (resid_ready, 2 * b + 1))
                before_x_dbl = ((xn_sb, 2 * b) if not first else None, None, None, (xn_sb, 2 * b + 1))
                for s in range(NG):
                    for n in range(STATES):
                        if n not in POOL_C[s]:
                            broadcast_c(b, s, n)
                        if not (last and s == NG - 1):
                            for a in range(DT):
                                if n == LATER_STAGES[f"u{a}"]:
                                    make_u(*following(b, s), a)
                        if n == CONVOLVE[s] and not (last and s >= NG - 2):
                            convolve(*following(*following(b, s)), before_conv[s])
                        if s == NG - 1 or (s == 0 and not first):
                            of, h_e = (b, 0) if s else (b - 1, 1)
                            if n == CLOSING["output"]:
                                output_product(of, h_e, last and s == NG - 1)
                            if n == CLOSING["transpose"]:
                                transpose_norm(of, h_e)
                        for j in range(DT * CHUNKS):
                            if n == PROJECTIONS[f"z{j}"] and s == j // 2:
                                project_z(b, j, first)
                        if s == 1 and not last:
                            for c in range(CHUNKS):
                                if n == PROJECTIONS[f"h{c}"]:
                                    transpose_h(b + 1, c)
                        if s == 2 and not last:
                            for j in range(DT * CHUNKS):
                                if n == PROJECTIONS[f"x{j}"]:
                                    project_x(b + 1, j)
                        if n == FIRST_STAGES["x_dbl"] and not (last and s >= NG - 2):
                            make_x_dbl(*following(*following(b, s)), before_x_dbl[s])
                        if n < 2 and s:
                            add_state(b, s - 1, n - 2 + STATES)
                        elif n < 2 and not first:
                            add_state(b - 1, NG - 1, n - 2 + STATES)
                        if n == CLOSING["start sum"]:
                            start_sum(b, s, first)
                        for m in ADDED_AT[n]:
                            add_state(b, s, m)

            transpose_h(0, 0)
            transpose_h(0, 1)
            transpose_w_in()
            pe.wait_ge(weights_sb, 1)
            project_x(0, 0)
            project_x(0, 1)
            convolve(0, 0, (pads_ready, 5))
            transpose_weights()
            project_x(0, 2)
            project_x(0, 3)
            pe.wait_ge(weights_sb, 4)
            pe.wait_ge(select_ready, 1)
            make_x_dbl(0, 0, (weights_sb, 4))
            make_u(0, 0, 0)
            pe.wait_ge(x_sb, DT * CHUNKS)
            make_u(0, 0, 1)
            pe.wait_ge(select_ready, 1)
            convolve(0, 1, (u_taken, 4))
            make_x_dbl(0, 1)
            batches(pe, batch)
            add_state(BATCH - 1, NG - 1, STATES - 2)
            add_state(BATCH - 1, NG - 1, STATES - 1)
            output_product(BATCH - 1, 1, True)
            transpose_norm(BATCH - 1, 1)
            pe.wait_ge(wq_ready, 1)
            pe.wait_ge(xn_sb, 2 * BATCH)
            for j in range(2 * BATCH):
                pe.wait_ge(clipped, j + 1)
                bank = last_bank(j)
                for t in range(TT):
                    k = (j * TT + t) * P
                    ins = nc.tensor.matmul(bank[:, t * P:(t + 1) * P], xn_t[:, k:k + P], w_q[:], start=True, stop=True)
                ins.then_inc(out_ps, 1)


_NAMES = ["L0_attn_hidden_states", "L0_attn_W_in", "L0_attn_W_out", "L0_attn_conv_w_fwd", "L0_attn_conv_b_fwd",
          "L0_attn_Wx_fwd", "L0_attn_Wdt_fwd", "L0_attn_bdt_fwd", "L0_attn_A_log_fwd", "L0_attn_D_fwd",
          "L0_attn_conv_w_rev", "L0_attn_conv_b_rev", "L0_attn_Wx_rev", "L0_attn_Wdt_rev", "L0_attn_bdt_rev",
          "L0_attn_A_log_rev", "L0_attn_D_rev", "L0_ffn_weight", "L0_ffn_ln_gamma", "L0_ffn_ln_beta"]


def kernel(**inputs):
    import numpy as np
    import concourse.bacc as bacc
    from concourse.bass_utils import run_bass_kernel_spmd

    nc = bacc.Bacc("TRN2", target_bir_lowering=False, num_devices=1)
    arrays, args = {}, []
    for name in _NAMES:
        a = np.ascontiguousarray(inputs[name])
        arrays[f"in_{name}"] = a
        args.append(nc.dram_tensor(f"in_{name}", a.shape, mybir.dt.from_np(a.dtype), kind="ExternalInput").ap())
    args.append(nc.dram_tensor("out", (BATCH, SEQ, MODEL), mybir.dt.float32, kind="ExternalOutput").ap())
    build(nc, *args)
    r = run_bass_kernel_spmd(nc, [arrays], core_ids=[0])
    return r.results[0]["out"]
```
